# Optimizing a Trainium2 kernel written in Bass

```python
import numpy as np
import jax
import jax.numpy as jnp

def _softmax(x, axis=-1):
    return jax.nn.softmax(x, axis=axis)

def _gelu(x):
    return jax.nn.gelu(x, approximate=True)

def _silu(x):
    return jax.nn.silu(x)

def _sigmoid(x):
    return jax.nn.sigmoid(x)

def _layernorm(x, axis=-1, eps=1e-05):
    m = jnp.mean(x, axis=axis, keepdims=True)
    v = jnp.var(x, axis=axis, keepdims=True)
    return (x - m) / jnp.sqrt(v + eps)

def _scatter_add(tgt, idx, src, axis=0):
    return tgt.at[idx].add(src)

def _segment_sum(src, seg, n):
    return jax.ops.segment_sum(src, seg, n)
kernel_name = 'mk_lm_tower_d1_tok_ids4096_r4_ae824a'

def setup_inputs(seed: int=0):
    np.random.seed(seed)
    _w = jnp.asarray

    def _rec_inputs():
        import jax
        import jax.numpy as jnp
        _rk = jax.random.key(seed)
        x = jax.random.randint(jax.random.fold_in(_rk, 1), (4, 1024), 0, 31993, jnp.int32)
        mask_BS_i1_0 = jnp.where(jnp.ones((4, 1024), dtype=bool), 1, 0).astype(jnp.int32)
        mask_BS_i0_1 = jnp.where(jnp.ones((4, 1024), dtype=bool), 0, 1).astype(jnp.int32)
        return (x, mask_BS_i1_0, mask_BS_i0_1)
    x, mask_BS_i1_0, mask_BS_i0_1 = _rec_inputs()

    def _L0_tok_setup():
        import jax, jax.numpy as jnp
        import numpy as np
        V, D, R = (8000, 1024, 128)
        B, S = (2, 1024)
        SCALE = 2.0
        PAD = 0
        key = jax.random.key(seed)
        ks = jax.random.split(key, 12)
        inp = {'x': jax.random.randint(ks[0], (B, S), 0, V, dtype=jnp.int32), 'cl_mask': jax.random.randint(ks[1], (B, S), 0, 2, dtype=jnp.int32), 'lm_mask': jax.random.randint(ks[2], (B, S), 0, 2, dtype=jnp.int32), 'cl_prime_mask': jax.random.randint(ks[3], (B, S), 0, 2, dtype=jnp.int32), 'weight': jax.random.normal(ks[4], (V, D), dtype=jnp.float32) * 0.02, 'lora_A_cl': jax.random.normal(ks[5], (V, R), dtype=jnp.float32) * 0.02, 'lora_B_cl': jax.random.normal(ks[6], (R, D), dtype=jnp.float32), 'lora_A_lm': jax.random.normal(ks[7], (V, R), dtype=jnp.float32) * 0.02, 'lora_B_lm': jax.random.normal(ks[8], (R, D), dtype=jnp.float32), 'lora_A_cl_prime': jax.random.normal(ks[9], (V, R), dtype=jnp.float32) * 0.02, 'lora_B_cl_prime': jax.random.normal(ks[10], (R, D), dtype=jnp.float32)}
        return inp
    _L0_tok_all = _L0_tok_setup()
    _L0_tok_in = {k: v for k, v in _L0_tok_all.items() if k in ('weight', 'lora_A_cl', 'lora_B_cl', 'lora_A_lm', 'lora_B_lm', 'lora_A_cl_prime', 'lora_B_cl_prime')}
    del _L0_tok_all

    def _L0_attn_setup():
        import jax, jax.numpy as jnp
        import numpy as np
        B, S, HID = (1, 512, 1024)
        NH, NKV = (32, 8)
        HD = HID // NH
        GROUPS = NH // NKV
        ROPE_THETA = 10000.0

        def _rope_cos_sin(seq_len, head_dim, dtype=jnp.float32):
            inv_freq = 1.0 / ROPE_THETA ** (jnp.arange(0, head_dim, 2, dtype=jnp.float32) / head_dim)
            t = jnp.arange(seq_len, dtype=jnp.float32)
            freqs = jnp.outer(t, inv_freq)
            emb = jnp.concatenate([freqs, freqs], axis=-1)
            return (jnp.cos(emb).astype(dtype), jnp.sin(emb).astype(dtype))

        def _rotate_half(x):
            x1, x2 = jnp.split(x, 2, axis=-1)
            return jnp.concatenate([-x2, x1], axis=-1)

        def _apply_rope(x, cos, sin):
            return x * cos[None, None] + _rotate_half(x) * sin[None, None]
        key = jax.random.key(seed)
        k1, k2, k3, k4, k5 = jax.random.split(key, 5)
        return {'hidden_states': jax.random.normal(k1, (B, S, HID), jnp.float32), 'Wq': jax.random.normal(k2, (NH * HD, HID), jnp.float32) * 0.02, 'Wk': jax.random.normal(k3, (NKV * HD, HID), jnp.float32) * 0.02, 'Wv': jax.random.normal(k4, (NKV * HD, HID), jnp.float32) * 0.02, 'Wo': jax.random.normal(k5, (HID, NH * HD), jnp.float32) * 0.02}
    _L0_attn_all = _L0_attn_setup()
    _L0_attn_in = {k: v for k, v in _L0_attn_all.items() if k in ('Wq', 'Wk', 'Wv', 'Wo')}
    del _L0_attn_all

    def _L0_ffn_setup():
        import jax, jax.numpy as jnp
        import numpy as np
        B, L, H, Dh, M = (4, 512, 16, 64, 256)
        D = H * Dh
        key = jax.random.key(seed)
        kx, ku, kd, kp = jax.random.split(key, 4)
        x = jax.random.normal(kx, (B, L, D), dtype=jnp.float32)
        up = jax.random.normal(ku, (H, Dh, M), dtype=jnp.float32)
        down = jax.random.normal(kd, (H, M, Dh), dtype=jnp.float32)
        perm = jax.random.permutation(kp, D)
        return {'x': x, 'up': up, 'down': down, 'perm': perm}
    _L0_ffn_all = _L0_ffn_setup()
    _L0_ffn_in = {k: v for k, v in _L0_ffn_all.items() if k in ('up', 'down', 'perm')}
    del _L0_ffn_all
    return {'x': x, 'mask_BS_i1_0': mask_BS_i1_0, 'mask_BS_i0_1': mask_BS_i0_1, 'L0_tok_weight': _L0_tok_in['weight'], 'L0_tok_lora_A_cl': _L0_tok_in['lora_A_cl'], 'L0_tok_lora_B_cl': _L0_tok_in['lora_B_cl'], 'L0_tok_lora_A_lm': _L0_tok_in['lora_A_lm'], 'L0_tok_lora_B_lm': _L0_tok_in['lora_B_lm'], 'L0_tok_lora_A_cl_prime': _L0_tok_in['lora_A_cl_prime'], 'L0_tok_lora_B_cl_prime': _L0_tok_in['lora_B_cl_prime'], 'L0_attn_Wq': _L0_attn_in['Wq'], 'L0_attn_Wk': _L0_attn_in['Wk'], 'L0_attn_Wv': _L0_attn_in['Wv'], 'L0_attn_Wo': _L0_attn_in['Wo'], 'L0_ffn_up': _L0_ffn_in['up'], 'L0_ffn_down': _L0_ffn_in['down'], 'L0_ffn_perm': _L0_ffn_in['perm']}

def reference(x, mask_BS_i1_0, mask_BS_i0_1, L0_tok_weight, L0_tok_lora_A_cl, L0_tok_lora_B_cl, L0_tok_lora_A_lm, L0_tok_lora_B_lm, L0_tok_lora_A_cl_prime, L0_tok_lora_B_cl_prime, L0_attn_Wq, L0_attn_Wk, L0_attn_Wv, L0_attn_Wo, L0_ffn_up, L0_ffn_down, L0_ffn_perm):
    import jax
    import jax.numpy as jnp

    def _L0_tok_ref(x, cl_mask, lm_mask, cl_prime_mask, weight, lora_A_cl, lora_B_cl, lora_A_lm, lora_B_lm, lora_A_cl_prime, lora_B_cl_prime):
        import jax, jax.numpy as jnp
        import numpy as np
        V, D, R = (8000, 1024, 128)
        B, S = (2, 1024)
        SCALE = 2.0
        PAD = 0
        result = weight[x]
        for A, Bm, m in ((lora_A_cl, lora_B_cl, cl_mask), (lora_A_lm, lora_B_lm, lm_mask), (lora_A_cl_prime, lora_B_cl_prime, cl_prime_mask)):
            after_A = A[x * m]
            result = result + SCALE * jnp.einsum('bsr,rd->bsd', after_A, Bm)
        return result

    def _L0_attn_ref(hidden_states, Wq, Wk, Wv, Wo):
        import jax, jax.numpy as jnp
        import numpy as np
        B, S, HID = (1, 512, 1024)
        NH, NKV = (32, 8)
        HD = HID // NH
        GROUPS = NH // NKV
        ROPE_THETA = 10000.0

        def _rope_cos_sin(seq_len, head_dim, dtype=jnp.float32):
            inv_freq = 1.0 / ROPE_THETA ** (jnp.arange(0, head_dim, 2, dtype=jnp.float32) / head_dim)
            t = jnp.arange(seq_len, dtype=jnp.float32)
            freqs = jnp.outer(t, inv_freq)
            emb = jnp.concatenate([freqs, freqs], axis=-1)
            return (jnp.cos(emb).astype(dtype), jnp.sin(emb).astype(dtype))

        def _rotate_half(x):
            x1, x2 = jnp.split(x, 2, axis=-1)
            return jnp.concatenate([-x2, x1], axis=-1)

        def _apply_rope(x, cos, sin):
            return x * cos[None, None] + _rotate_half(x) * sin[None, None]
        bsz, q_len, _ = hidden_states.shape
        q = (hidden_states @ Wq.T).reshape(bsz, q_len, NH, HD).transpose(0, 2, 1, 3)
        k = (hidden_states @ Wk.T).reshape(bsz, q_len, NKV, HD).transpose(0, 2, 1, 3)
        v = (hidden_states @ Wv.T).reshape(bsz, q_len, NKV, HD).transpose(0, 2, 1, 3)
        cos, sin = _rope_cos_sin(q_len, HD, hidden_states.dtype)
        q = _apply_rope(q, cos, sin)
        k = _apply_rope(k, cos, sin)
        k = jnp.repeat(k, GROUPS, axis=1)
        v = jnp.repeat(v, GROUPS, axis=1)
        scale = 1.0 / jnp.sqrt(jnp.asarray(HD, hidden_states.dtype))
        logits = jnp.einsum('bhqd,bhkd->bhqk', q, k) * scale
        causal = jnp.tril(jnp.ones((q_len, q_len), dtype=bool))
        logits = jnp.where(causal[None, None], logits, jnp.finfo(logits.dtype).min)
        attn = jax.nn.softmax(logits, axis=-1)
        out = jnp.einsum('bhqk,bhkd->bhqd', attn, v)
        out = out.transpose(0, 2, 1, 3).reshape(bsz, q_len, NH * HD)
        return out @ Wo.T

    def _L0_ffn_ref(x, up, down, perm):
        import jax, jax.numpy as jnp
        import numpy as np
        B, L, H, Dh, M = (4, 512, 16, 64, 256)
        D = H * Dh
        b, l, Dm = x.shape
        h, d = (up.shape[0], up.shape[1])
        unperm = jnp.argsort(perm)
        t = x.reshape(b * l, Dm)
        t = t[:, perm]
        t = t.reshape(b * l, h, d)
        t = jnp.einsum('bhd,hdm->bhm', t, up)
        t = jax.nn.gelu(t, approximate=False)
        t = jnp.einsum('bhm,hmd->bhd', t, down)
        t = t.reshape(b * l, h * d)
        t = t[:, unperm]
        out = t.reshape(b, l, Dm)
        return out
    h = _L0_tok_ref(x, mask_BS_i1_0, mask_BS_i0_1, mask_BS_i0_1, L0_tok_weight, L0_tok_lora_A_cl, L0_tok_lora_B_cl, L0_tok_lora_A_lm, L0_tok_lora_B_lm, L0_tok_lora_A_cl_prime, L0_tok_lora_B_cl_prime)
    h = h + _L0_attn_ref(_layernorm(h, axis=-1), L0_attn_Wq, L0_attn_Wk, L0_attn_Wv, L0_attn_Wo)
    h = h + _L0_ffn_ref(_layernorm(h, axis=-1), L0_ffn_up, L0_ffn_down, L0_ffn_perm)
    return h

_drawn_inputs = setup_inputs


def setup_inputs(seed=0):
    import zlib

    import numpy as np

    out = dict(_drawn_inputs(seed))
    spreads = {}
    factors = {'L0_attn_Wq': 5.206, 'L0_attn_Wk': 5.036}
    for name, (base, spread) in spreads.items():
        noise = np.random.default_rng([zlib.crc32(name.encode()), seed]).standard_normal(out[name].shape)
        drawn = base * np.exp(spread * noise) if base else spread * noise
        out[name] = jnp.asarray(drawn.astype(out[name].dtype))
    for name, factor in factors.items():
        out[name] = (out[name] * factor).astype(out[name].dtype)
    return out
```

```python
import concourse.bass as bass
from concourse import mybir
from contextlib import ExitStack

F32 = mybir.dt.float32
F32R = mybir.dt.float32r
I32 = mybir.dt.int32
ALU = mybir.AluOpType
ACT = mybir.ActivationFunctionType
AX_X = mybir.AxisListType.X

P = 128
B, S, D = 4, 1024, 1024
V, R = 8000, 128
NH, NKV = 32, 8
HD = D // NH
GQ = NH // NKV
T = S // P
KT = D // P
H = S // 2
FH, FD, FM = 16, 64, 256
MT = 2 + NKV
SCALE = float(HD) ** -0.5
EPS = 1e-5
NEG = -3.0e38

C_B, C_V, C_M, C_O, C_U, NCHUNK = 0, 4, 6, 16, 24, 28
STEPS = [(qh, kt) for qh in range(2) for kt in range(4 * (qh + 1))]
NSTEP = len(STEPS)
DIAG = [n for n, (qh, kt) in enumerate(STEPS) if kt >= 4 * qh]
PIECES = [(qt, kh, jp) for qt in range(T) for kh in range(qt // 4 + 1) for jp in range(2)]
NPIECE = len(PIECES)
MASKED = [n for n, (qt, kh, jp) in enumerate(PIECES) if kh == qt // 4]
SPREAD = {2: 3, 3: 3, 4: 2, 5: 3, 6: 3, 7: 2, 8: 3, 9: 3, 10: 2}
LAG = 2


def step_range(n):
    qh, kt = STEPS[n]
    q0 = max(H * qh, P * kt)
    return q0, H * (qh + 1) - q0


def pieces_of(n):
    first = sum(c for k, c in SPREAD.items() if k < n)
    return list(range(first, first + SPREAD.get(n, 0)))


def program(nc, ids, mask1, mask0, table_w, table_a1, table_a23, chunks, down, cos, sin, perm_up, perm_down, out):
    with ExitStack() as ctx:
        def sb(name, shape, dt=F32):
            return ctx.enter_context(nc.sbuf_tensor(name, shape, dt))

        def sem(name):
            return ctx.enter_context(nc.semaphore(name))

        qk_dram = nc.dram_tensor("qk_dram", (2, MT * P, S), F32, kind="Internal").ap()
        y_dram = nc.dram_tensor("y_dram", (2 * D, S), F32, kind="Internal").ap()
        z_dram = nc.dram_tensor("z_dram", (D, S), F32, kind="Internal").ap()
        m_dram = nc.dram_tensor("m_dram", (2, 2, GQ * T, P), F32, kind="Internal").ap()

        h = sb("h", [P, T, D])
        x_hi = sb("x_hi", [P, KT, S], F32R)
        x_lo = sb("x_lo", [P, KT, S], F32R)
        ring = sb("ring", [P, 8, 1024], F32R)
        kst = sb("kst", [P, 2, S], F32R)
        work = sb("work", [P, 3, GQ, H])
        v_all = sb("v_all", [P, T, NKV * HD])
        vg = sb("vg", [P, 2, T, HD])
        raw = sb("raw", [P, 2, 1024])
        cos_sb = sb("cos_sb", [P, S])
        sin_sb = sb("sin_sb", [P, S])
        a_rows = sb("a_rows", [P, 2, 3 * R])
        attn = sb("attn", [P, 2, H])
        rden = sb("rden", [P, H])
        ident = sb("ident", [P, P])
        causal = sb("causal", [P, P])
        ones = sb("ones", [P, HD])
        stats = sb("stats", [P, T, 2, 6])
        mv = sb("mv", [P, T, 2])
        ve = sb("ve", [P, T])
        sd = sb("sd", [P, T])
        rstd = sb("rstd", [P, T])
        nwt = sb("nwt", [P, T])
        mx = sb("mx", [P, 2, GQ, T, 2])
        negm = sb("negm", [P, 2, GQ * T])
        m_hi = sb("m_hi", [GQ * T, 2, P], F32R)
        m_lo = sb("m_lo", [GQ * T, 2, P], F32R)
        idx_raw = sb("idx_raw", [P, 3, B * T], I32)
        idx_neg = sb("idx_neg", [P, 3, B * T], I32)
        idx_all = sb("idx_all", [P, B * T, 3], I32)
        idx_now = sb("idx_now", [P, 2, 3], I32)
        pu = sb("pu", [P, FH], I32)
        pu_now = sb("pu_now", [P, 2, 1], I32)
        pd = sb("pd", [P, FH // 2], I32)
        pd_now = sb("pd_now", [P, 2, 1], I32)
        ps = ctx.enter_context(nc.psum_tensor("ps", [P, 8, 512], F32))

        flat = work[:].rearrange("p a j n -> p (a j n)")
        w_rows = flat[:, 0:2048].rearrange("p (u n) -> p u n", u=2)
        y = flat[:, 2048:4096].rearrange("p (u n) -> p u n", u=2)
        r_cos = flat[:, 0:1024].rearrange("p (u n) -> p u n", u=2)
        r_sin = flat[:, 1024:2048].rearrange("p (u n) -> p u n", u=2)
        r_swap = flat[:, 2048:3072].rearrange("p (u n) -> p u n", u=2)
        gel = flat[:, 0:4096].rearrange("p (a m n) -> p a m n", a=4, m=2)
        d_out = flat[:, 4096:6144].rearrange("p (u n) -> p u n", u=2)
        kflat = kst[:].rearrange("p u n -> p (u n)")
        a_t = kflat[:, 0:1536].rearrange("p (u x n) -> p u x n", u=2, x=2)
        r_hi = kflat[:, 0:1024].rearrange("p (u n) -> p u n", u=2)
        r_lo = kflat[:, 1024:2048].rearrange("p (u n) -> p u n", u=2)
        down_sb = v_all[:].rearrange("p t n -> p (t n)")
        z_sb = x_hi[:].bitcast(F32)

        def hi(s):
            return ring[:, 2 * s, :]

        def lo(s):
            return ring[:, 2 * s + 1, :]

        def f32(ap):
            return ap.bitcast(F32)

        loaded = sem("loaded")
        consts = sem("consts")
        idx_ok = sem("idx_ok")
        prep = sem("prep")
        raw_in = [sem(f"raw_in{u}") for u in range(2)]
        w_hi = sem("w_hi")
        w_lo = sem("w_lo")
        idx_cp = sem("idx_cp")
        gathered = [sem(f"gathered{u}") for u in range(2)]
        at_ps = sem("at_ps")
        at_hi = sem("at_hi")
        at_lo = sem("at_lo")
        emb_ps = sem("emb_ps")
        h_set = sem("h_set")
        st_set = sem("st_set")
        mv_set = sem("mv_set")
        ln_ve = sem("ln_ve")
        ln_sd = sem("ln_sd")
        ln_nw = sem("ln_nw")
        y_set = sem("y_set")
        y_ps = sem("y_ps")
        y_hi = sem("y_hi")
        y_lo = sem("y_lo")
        v_ps = sem("v_ps")
        v_set = sem("v_set")
        p_ps = sem("p_ps")
        p_cos = sem("p_cos")
        p_sin = sem("p_sin")
        swapped = [sem(f"swapped{u}") for u in range(2)]
        p_add = sem("p_add")
        p_hi = sem("p_hi")
        p_lo = sem("p_lo")
        p_out = [sem(f"p_out{u}") for u in range(2)]
        k_ones = sem("k_ones")
        qk_in = [sem(f"qk_in{u}") for u in range(2)]
        mx_ps = sem("mx_ps")
        mx_mk = sem("mx_mk")
        mx_rd = sem("mx_rd")
        m_neg = sem("m_neg")
        m_ps = sem("m_ps")
        m_h = sem("m_h")
        m_row = sem("m_row")
        m_st = sem("m_st")
        m_in = sem("m_in")
        st_ps = sem("st_ps")
        e_set = sem("e_set")
        e_mask = sem("e_mask")
        vg_set = sem("vg_set")
        o_ps = sem("o_ps")
        o_rd = sem("o_rd")
        o_nm = sem("o_nm")
        o_hi = sem("o_hi")
        o_lo = sem("o_lo")
        op_ps = sem("op_ps")
        op_set = sem("op_set")
        y_out = sem("y_out")
        down_in = sem("down_in")
        pu_cp = sem("pu_cp")
        t_in = [sem(f"t_in{u}") for u in range(2)]
        up_ps = sem("up_ps")
        gel_set = sem("gel_set")
        dn_ps = sem("dn_ps")
        dn_set = sem("dn_set")
        pd_cp = sem("pd_cp")
        z_out = [sem(f"z_out{u}") for u in range(2)]
        z_in = sem("z_in")
        f_ps = sem("f_ps")
        f_set = sem("f_set")
        stored = sem("stored")
        gate_pool = sem("gate_pool")
        gate_act = sem("gate_act")
        gate_dve = sem("gate_dve")
        gate_pe = sem("gate_pe")
        gate_sp = sem("gate_sp")

        block = ctx.enter_context(nc.Block())

        @block.sync
        def _(sp):
            def gate(s, value):
                sp.wait_ge(s, value)
                sp.sem_inc(gate_sp, 1)

            for dst, src in ((idx_raw[:, 0, :], ids), (idx_raw[:, 1, :], mask1), (idx_raw[:, 2, :], mask0),
                             (cos_sb[:], cos), (sin_sb[:], sin), (pu[:], perm_up), (pd[:], perm_down)):
                sp.dma_start(dst, src).then_inc(loaded, 16)

            def load_chunk(b, c, u):
                gate(w_lo, b * NCHUNK + c + 1)
                sp.dma_start(raw[:, u, :], chunks[bass.ds(c, 1), :, :].rearrange("o p n -> (o p) n")).then_inc(raw_in[u], 16)

            def load_group(b, g, u):
                for row, half in ((0, 0), (1, 1), (2, 0)):
                    sp.dma_start(f32(ring[HD * row:HD * row + HD, 4 * u:4 * u + GQ, :]),
                                 qk_dram[half, bass.ds((2 + g) * P, P), :].rearrange("(j d) n -> d j n", d=HD)).then_inc(qk_in[u], 16)
                for row, half in ((0, 0), (1, 0), (2, 1)):
                    sp.dma_start(f32(kst[HD * row:HD * row + HD, u, :]),
                                 qk_dram[half, bass.ds(g * HD, HD), :]).then_inc(qk_in[u], 16)

            def max_rows(gi, u):
                gate(m_row, gi + 2)
                sp.dma_start(m_dram[0, u, :, :], f32(m_hi[:, u, :])).then_inc(m_st, 16)
                sp.dma_start(m_dram[1, u, :, :], f32(m_lo[:, u, :])).then_inc(m_st, 16)
                gate(m_st, (gi + 1) * 32)
                for x in range(2):
                    sp.dma_start(f32(ring[96 + x:97 + x, 4 * u:4 * u + GQ, :]),
                                 m_dram[x, bass.ds(u, 1), :, :].rearrange("o (j t) n -> o j (t n)", j=GQ)).then_inc(m_in, 16)

            with sp.Fori(0, B) as b:
                for c in range(6):
                    load_chunk(b, c, c % 2)
                for c in range(6, 10):
                    load_chunk(b, c, c % 2)
                def rotate_and_store(m):
                    for hf in range(2):
                        r = (b * MT + m) * 2 + hf
                        gate(p_sin, r + 1)
                        gate(p_add, r + 1)
                        sp.dma_start(r_swap[0:P:2, hf, :], r_sin[1:P:2, hf, :]).then_inc(swapped[hf], 16)
                        sp.dma_start(r_swap[1:P:2, hf, :], r_sin[0:P:2, hf, :]).then_inc(swapped[hf], 16)
                    for hf in range(2):
                        gate(p_lo, (b * MT + m) * 2 + hf + 3)
                        for x, src in ((0, r_hi), (1, r_lo)):
                            sp.dma_start(qk_dram[x, bass.ds(m * P, P), H * hf:H * hf + H], f32(src[:, hf, :])).then_inc(p_out[hf], 16)

                with sp.Fori(0, MT // 2 - 1) as mm:
                    for u in range(2):
                        rotate_and_store(mm * 2 + u)
                        load_chunk(b, mm * 2 + u + 10, u)
                for u in range(2):
                    rotate_and_store(MT - 2 + u)
                for u in range(2):
                    gate(p_out[u], (b + 1) * (MT * 32) + 32)
                load_group(b, 0, 0)
                load_group(b, 1, 1)
                max_rows(b * NKV, 0)

                def group(g, u):
                    max_rows(b * NKV + g + 1, 1 - u)
                    gate(st_ps, (b * NKV + g + 1) * NSTEP)
                    load_group(b, g + 2, u)

                with sp.Fori(0, 3) as gg:
                    for u in range(2):
                        group(gg * 2 + u, u)
                max_rows(b * NKV + 7, 1)
                gate(o_ps, (b + 1) * (2 * NKV))
                sp.dma_start(down_sb, down).then_inc(down_in, 16)
                for c in range(18, 20):
                    load_chunk(b, c, c % 2)
                with sp.Fori(0, 4) as n:
                    for u in range(2):
                        load_chunk(b, n * 2 + u + 20, u)
                gate(y_lo, (b * 2 + 2) * T + 2)
                for x, src in enumerate((x_hi, x_lo)):
                    sp.dma_start(y_dram[D * x:D * x + D, :].rearrange("(k p) n -> p k n", p=P), f32(src[:])).then_inc(y_out, 16)
                for u in range(2):
                    gate(z_out[u], (b + 1) * (16 * FH // 4))
                gate(y_out, (b + 1) * 32)
                sp.dma_start(z_sb, z_dram.rearrange("(k p) n -> p k n", p=P)).then_inc(z_in, 16)
                with sp.Fori(0, T) as t:
                    gate(f_set, b * T + t + 3)
                    sp.dma_start(out[bass.ds((b * T + t) * P, P), :],
                                 h[:, bass.ds(t, 1), :].rearrange("p o n -> p (o n)")).then_inc(stored, 16)
            sp.wait_ge(stored, 16 * B * T)

        @block.gpsimd
        def _(pool):
            pool.sem_inc(w_lo, 2)
            pool.sem_inc(p_add, 2)
            pool.sem_inc(p_lo, 2)
            pool.sem_inc(o_lo, 2)
            pool.memset(ident[:], 0.0).then_inc(consts, 1)
            pool.memset(causal[:], 0.0).then_inc(consts, 1)
            pool.memset(ones[:], 1.0).then_inc(consts, 1)
            pool.wait_ge(consts, 3)
            pool.affine_select(out=ident[:], in_=ident[:], compare_op=ALU.not_equal, fill=1.0, base=0,
                               pattern=[[-1, P]], channel_multiplier=1).then_inc(consts, 1)
            pool.affine_select(out=causal[:], in_=causal[:], compare_op=ALU.is_ge, fill=NEG, base=0,
                               pattern=[[-1, P]], channel_multiplier=1).then_inc(consts, 1)
            pool.wait_ge(idx_ok, 1)

            def gate(s, value):
                pool.wait_ge(s, value)
                pool.sem_inc(gate_pool, 1)

            def split_lo(b, c, s, u):
                gate(w_hi, b * NCHUNK + c + 1)
                pool.tensor_tensor(lo(s), raw[:, u, :], f32(hi(s)), ALU.subtract).then_inc(w_lo, 1)

            with pool.Fori(0, B) as b:
                for c in range(4):
                    split_lo(b, C_B + c, c, c % 2)
                with pool.Fori(0, T // 2) as tt:
                    for u in range(2):
                        n = b * T + tt * 2 + u
                        gate(h_set, n + 1)
                        pool.tensor_copy(idx_now[:, u, :], idx_all[:, bass.ds(n, 1), :].rearrange("p o i -> p (o i)")).then_inc(idx_cp, 1)
                        gate(idx_cp, n + 1)
                        for k, (dst, table, rows) in enumerate(((w_rows[:, u, :], table_w, V), (a_rows[:, u, 0:R], table_a1, V),
                                                               (a_rows[:, u, R:3 * R], table_a23, V))):
                            pool.indirect_dma_start(dst, None, table, bass.IndirectOffsetOnAxis(ap=idx_now[:, u, k:k + 1], axis=0)).then_inc(gathered[u], 16)
                for c, s in ((4, 0), (5, 1), (6, 2), (7, 3)):
                    split_lo(b, c, s, c % 2)

                def rotate(m):
                    for hf in range(2):
                        r = (b * MT + m) * 2 + hf
                        gate(swapped[hf], (b * MT + m + 1) * 32)
                        pool.tensor_tensor(r_cos[:, hf, :], r_cos[:, hf, :], r_swap[:, hf, :], ALU.add).then_inc(p_add, 1)
                        gate(p_hi, r + 1)
                        pool.tensor_tensor(r_lo[:, hf, :], r_cos[:, hf, :], f32(r_hi[:, hf, :]), ALU.subtract).then_inc(p_lo, 1)

                with pool.Fori(0, MT // 2 - 1) as mm:
                    for u in range(2):
                        rotate(mm * 2 + u)
                        split_lo(b, mm * 2 + u + 8, 2 + u, u)
                for u in range(2):
                    rotate(MT - 2 + u)
                for u in range(2):
                    gate(p_out[u], (b + 1) * (MT * 32) + 32)
                pool.memset(f32(kst[96:98, :, :]), 1.0).then_inc(k_ones, 1)
                gate(k_ones, b + 1)

                def values(g, u):
                    pool.tensor_copy(vg[:, u, :, :], v_all[:, :, bass.ds(g * HD, HD)]).then_inc(vg_set, 1)

                def group(g, u, first=False, last=False):
                    gi = b * NKV + g
                    for n in range(NSTEP):
                        if n in DIAG:
                            gate(e_set, gi * NSTEP + n + 2)
                            pool.affine_select(out=work[:, n % 3, :, 0:P], in_=work[:, n % 3, :, 0:P], compare_op=ALU.is_ge,
                                               fill=0.0, base=0, pattern=[[0, GQ], [1, P]], channel_multiplier=-1).then_inc(e_mask, 1)
                        if n == 2 and not first:
                            split_attn(g - 1, 1)
                        if n == 3 and not last:
                            if not first:
                                gate(o_ps, gi * 2)
                            values(g + 1, 1 - u)
                        if n == 8:
                            split_attn(g, 0)

                def split_attn(g, qh):
                    k = (b * NKV + g) * 2 + qh
                    gate(o_hi, k + 1)
                    col = x_lo[:, bass.ds(g, 1), H * qh:H * qh + H].rearrange("p o n -> p (o n)")
                    src = x_hi[:, bass.ds(g, 1), H * qh:H * qh + H].rearrange("p o n -> p (o n)")
                    pool.tensor_tensor(col, attn[:, qh, :], f32(src), ALU.subtract).then_inc(o_lo, 1)

                gate(v_set, (b + 1) * T + 4)
                values(0, 0)
                group(0, 0, first=True)
                with pool.Fori(0, 3) as gg:
                    group(gg * 2 + 1, 1)
                    group(gg * 2 + 2, 0)
                group(7, 1, last=True)
                split_attn(7, 1)

                for c in range(16, 20):
                    split_lo(b, c, c - 16, c % 2)
                with pool.Fori(0, 2) as nn:
                    for k in range(4):
                        split_lo(b, nn * 4 + 20 + k, k, k % 2)
                gate(y_out, (b + 1) * 32)

                def gather(hh, u):
                    pool.tensor_copy(pu_now[:, u, :], pu[:, bass.ds(hh, 1)]).then_inc(pu_cp, 1)
                    gate(pu_cp, b * FH + hh + 1)
                    pool.indirect_dma_start(f32(kst[:, u, :]), None, y_dram, bass.IndirectOffsetOnAxis(ap=pu_now[:, u, :], axis=0)).then_inc(t_in[u], 16)

                for u in range(2):
                    gather(u, u)
                for pp in range(FH // 2):
                    for u in range(2):
                        if pp < FH // 2 - 1:
                            gate(up_ps, b * (2 * FH) + (2 * pp + u) * 2 + 2)
                            gather(2 * pp + 2 + u, u)
                    gate(dn_set, b * (FH // 2) + pp + 3)
                    pool.tensor_copy(pd_now[:, pp % 2, :], pd[:, pp:pp + 1]).then_inc(pd_cp, 1)
                    gate(pd_cp, b * (FH // 2) + pp + 1)
                    pool.indirect_dma_start(z_dram, bass.IndirectOffsetOnAxis(ap=pd_now[:, pp % 2, :], axis=0),
                                            d_out[:, pp % 2, :], None).then_inc(z_out[pp % 2], 16)

        @block.scalar
        def _(act):
            act.sem_inc(v_set, 4)
            act.sem_inc(e_set, 1)
            act.sem_inc(gel_set, 2)

            def gate(s, value):
                act.wait_ge(s, value)
                act.sem_inc(gate_act, 1)

            def split_hi(b, pair, s, u):
                gate(raw_in[u], (b * (NCHUNK // 2) + pair + 1) * 16)
                act.activation(hi(s), raw[:, u, :], ACT.Copy).then_inc(w_hi, 1)

            def layernorm(b, which):
                act.wait_ge(ln_ve, b * 2 + which + 1)
                act.activation(sd[:], ve[:], ACT.Sqrt).then_inc(ln_sd, 1)
                with act.Fori(0, T // 2) as tt:
                    for u in range(2):
                        t = tt * 2 + u
                        gate(y_ps, (b * 2 + which) * T + t + 1)
                        act.activation(x_hi[:, :, bass.ds(t * P, P)],
                                       ps[:, 4 + 2 * u:6 + 2 * u, :].rearrange("p a (k n) -> p (a k) n", n=P), ACT.Copy).then_inc(y_hi, 1)

            with act.Fori(0, B) as b:
                for c in range(4):
                    split_hi(b, c // 2, c, c % 2)
                with act.Fori(0, T // 2) as tt:
                    for u in range(2):
                        act.wait_ge(at_ps, b * T + tt * 2 + u + 1)
                        act.activation(a_t[:, u, 0, :], ps[:, u, 0:3 * R], ACT.Copy).then_inc(at_hi, 1)
                act.wait_ge(emb_ps, (b + 1) * T)
                for c in range(4, 8):
                    split_hi(b, c // 2, c - 4, c % 2)
                layernorm(b, 0)
                for t in range(T):
                    act.wait_ge(v_ps, b * T + t + 1)
                    act.activation(v_all[:, t, :], ps[:, t % 4, 0:NKV * HD], ACT.Copy).then_inc(v_set, 1)

                def rotated_hi(m):
                    for hf in range(2):
                        gate(p_add, (b * MT + m) * 2 + hf + 3)
                        act.wait_ge(p_out[hf], (b * MT + m + 1) * 32)
                        act.activation(r_hi[:, hf, :], r_cos[:, hf, :], ACT.Copy).then_inc(p_hi, 1)

                with act.Fori(0, MT // 2 - 1) as mm:
                    for u in range(2):
                        rotated_hi(mm * 2 + u)
                        gate(p_ps, (b * MT + mm * 2 + u + 1) * 2)
                        split_hi(b, mm + 4, 2 + u, u)
                for u in range(2):
                    rotated_hi(MT - 2 + u)

                def group(g, first=False):
                    gi = b * NKV + g
                    for n in range(NSTEP):
                        w = step_range(n)[1]
                        act.wait_ge(st_ps, gi * NSTEP + n + 1)
                        act.activation(work[:, n % 3, :, 0:w], ps[:, 0:GQ, 0:w], ACT.Exp, scale=SCALE).then_inc(e_set, 1)
                        if n == 1 and not first:
                            attn_hi(g - 1, 1)
                        if n == 7:
                            attn_hi(g, 0)

                def attn_hi(g, qh):
                    gate(o_nm, (b * NKV + g) * 2 + qh + 2)
                    act.activation(x_hi[:, bass.ds(g, 1), H * qh:H * qh + H].rearrange("p o n -> p (o n)"),
                                   attn[:, qh, :], ACT.Copy).then_inc(o_hi, 1)

                group(0, first=True)
                with act.Fori(0, 3) as gg:
                    group(gg * 2 + 1)
                    group(gg * 2 + 2)
                group(7)
                attn_hi(7, 1)
                gate(st_ps, (b + 1) * (NKV * NSTEP))
                for c in range(16, 20):
                    split_hi(b, c // 2, c - 16, c % 2)
                with act.Fori(0, 2) as nn:
                    for k in range(4):
                        gate(op_ps, (b * 4 + nn * 2 + k // 2 + 1) * T)
                        split_hi(b, nn * 2 + 10 + k // 2, k, k % 2)
                layernorm(b, 1)
                for hh in range(FH):
                    for hf in range(2):
                        act.wait_ge(up_ps, b * (2 * FH) + 2 * hh + hf + 1)
                        if hh >= 2 and hf == 0:
                            act.wait_ge(dn_ps, b * (FH // 2) + hh // 2)
                        act.activation(gel[:, 2 * (hh % 2) + hf, :, :], ps[:, 2 * hf:2 * hf + 2, :], ACT.Gelu).then_inc(gel_set, 1)

        @block.vector
        def _(dve):
            v = nc.vector
            dve.sem_inc(h_set, 2)
            dve.sem_inc(y_lo, 2)
            dve.sem_inc(p_out[0], 32)
            dve.sem_inc(p_out[1], 32)
            dve.sem_inc(mx_rd, 1)
            dve.sem_inc(m_row, 1)
            dve.sem_inc(o_nm, 1)
            dve.sem_inc(op_set, 8)
            dve.sem_inc(dn_set, 2)
            dve.sem_inc(f_set, 2)

            def gate(s, value):
                dve.wait_ge(s, value)
                dve.sem_inc(gate_dve, 1)

            chain = [0]

            def link(ins):
                chain[0] += 1
                ins.then_inc(prep, 1)
                dve.wait_ge(prep, chain[0])

            dve.wait_ge(loaded, 7 * 16)
            link(v.memset(mx[:], NEG))
            link(v.tensor_tensor(idx_raw[:, 1, :], idx_raw[:, 1, :], idx_raw[:, 0, :], ALU.mult))
            link(v.tensor_tensor(idx_raw[:, 2, :], idx_raw[:, 2, :], idx_raw[:, 0, :], ALU.mult))
            link(v.tensor_scalar(idx_neg[:], idx_raw[:], 0, V, ALU.is_lt, ALU.mult))
            link(v.tensor_tensor(idx_raw[:], idx_raw[:], idx_neg[:], ALU.add))
            link(v.tensor_scalar(idx_all[:].rearrange("p n i -> p i n"), idx_raw[:], 0, V - 1, ALU.max, ALU.min))
            link(v.tensor_scalar(pu[FD:P, :], pu[FD:P, :], D, None, ALU.add))
            dve.wait_ge(consts, 5)
            dve.sem_inc(idx_ok, 1)

            def layernorm(b, which):
                ln = b * 2 + which
                with dve.Fori(0, T) as t:
                    for k in range(2):
                        v.bn_stats(out=stats[:, bass.ds(t, 1), k, :].rearrange("p o n -> p (o n)"),
                                   in_=h[:, bass.ds(t, 1), H * k:H * k + H].rearrange("p o n -> p (o n)")).then_inc(st_set, 1)
                gate(st_set, (ln + 1) * (2 * T))
                for t in range(T):
                    v.bn_aggr(out=mv[:, t, :], in_=stats[:, t, :, :].rearrange("p k s -> p (k s)")).then_inc(mv_set, 1)
                gate(mv_set, (ln + 1) * T)
                v.tensor_scalar(ve[:], mv[:, :, 1], EPS, None, ALU.add).then_inc(ln_ve, 1)
                gate(ln_sd, ln + 1)
                v.reciprocal(rstd[:], sd[:]).then_inc(ln_nw, 1)
                gate(ln_nw, ln * 5 + 1)
                v.tensor_tensor(nwt[:], rstd[:], rstd[:], ALU.mult).then_inc(ln_nw, 1)
                gate(ln_nw, ln * 5 + 2)
                v.tensor_tensor(nwt[:], nwt[:], ve[:], ALU.mult).then_inc(ln_nw, 1)
                gate(ln_nw, ln * 5 + 3)
                v.tensor_scalar(nwt[:], nwt[:], -0.5, 1.5, ALU.mult, ALU.add).then_inc(ln_nw, 1)
                gate(ln_nw, ln * 5 + 4)
                v.tensor_tensor(rstd[:], rstd[:], nwt[:], ALU.mult).then_inc(ln_nw, 1)
                gate(ln_nw, ln * 5 + 5)

                def normalise(t, u):
                    gate(y_lo, ln * T + t + 1)
                    v.tensor_scalar(y[:, u, :], h[:, bass.ds(t, 1), :].rearrange("p o n -> p (o n)"),
                                    mv[:, bass.ds(t, 1), 0:1].rearrange("p o n -> p (o n)"), rstd[:, bass.ds(t, 1)],
                                    ALU.subtract, ALU.mult).then_inc(y_set, 1)

                def split(t, u):
                    gate(y_hi, ln * T + t + 1)
                    cols = bass.ds(t * P, P)
                    v.tensor_tensor(x_lo[:, :, cols], ps[:, 4 + 2 * u:6 + 2 * u, :].rearrange("p a (k n) -> p (a k) n", n=P),
                                    f32(x_hi[:, :, cols]), ALU.subtract).then_inc(y_lo, 1)

                normalise(0, 0)
                normalise(1, 1)
                with dve.Fori(0, T // 2 - 1) as tt:
                    for u in range(2):
                        split(tt * 2 + u, u)
                        normalise(tt * 2 + u + 2, u)
                split(T - 2, 0)
                split(T - 1, 1)

            with dve.Fori(0, B) as b:
                with dve.Fori(0, T // 2) as tt:
                    for u in range(2):
                        n = b * T + tt * 2 + u
                        gate(at_hi, n + 1)
                        v.tensor_tensor(a_t[:, u, 1, :], ps[:, u, 0:3 * R], f32(a_t[:, u, 0, :]), ALU.subtract).then_inc(at_lo, 1)
                        gate(emb_ps, n + 1)
                        v.scalar_tensor_tensor(h[:, bass.ds(tt * 2 + u, 1), :].rearrange("p o n -> p (o n)"),
                                               ps[:, 2 + 2 * u:4 + 2 * u, :].rearrange("p a n -> p (a n)"), 2.0, w_rows[:, u, :],
                                               ALU.mult, ALU.add).then_inc(h_set, 1)
                gate(h_set, (b + 1) * T + 2)
                layernorm(b, 0)
                with dve.Fori(0, MT // 2) as mm:
                    for u in range(2):
                        for hf in range(2):
                            r = (b * MT + mm * 2 + u) * 2 + hf
                            gate(p_lo, r + 1)
                            gate(p_ps, r + 1)
                            bank = ps[:, 4 + 2 * u + hf, :]
                            v.tensor_tensor(r_cos[:, hf, :], bank, cos_sb[:, H * hf:H * hf + H], ALU.mult).then_inc(p_cos, 1)
                            v.tensor_tensor(r_sin[:, hf, :], bank, sin_sb[:, H * hf:H * hf + H], ALU.mult).then_inc(p_sin, 1)

                def maximum(g, u, k):
                    gi = b * NKV + g
                    qt, kh, jp = PIECES[k]
                    w = min(P * (qt + 1) - H * kh, H)
                    gate(mx_ps, gi * NPIECE + k + 1)
                    if k in MASKED:
                        diag = ps[:, 6:8, w - P:w]
                        v.tensor_tensor(diag, diag, causal[:].unsqueeze(1).to_broadcast([P, 2, P]), ALU.add).then_inc(mx_mk, 1)
                        gate(mx_mk, gi * len(MASKED) + MASKED.index(k) + 1)
                    v.tensor_reduce(out=mx[:, u, 2 * jp:2 * jp + 2, qt, kh:kh + 1], in_=ps[:, 6:8, 0:w], axis=AX_X, op=ALU.max).then_inc(mx_rd, 1)

                def minus_max(g, u):
                    gi = b * NKV + g
                    gate(mx_rd, (gi + 1) * NPIECE + 1)
                    v.tensor_reduce(out=negm[:, u, :], in_=mx[:, u, :, :, :].rearrange("p j t x -> p (j t) x"), axis=AX_X, op=ALU.max, negate=True).then_inc(m_neg, 1)
                    gate(m_ps, gi + 1)
                    v.tensor_copy(m_hi[:, u, :], ps[0:GQ * T, 6, 0:P]).then_inc(m_h, 1)
                    gate(m_h, gi + 1)
                    v.tensor_tensor(m_lo[:, u, :], ps[0:GQ * T, 6, 0:P], f32(m_hi[:, u, :]), ALU.subtract).then_inc(m_row, 1)

                def normalise_attn(g, qh):
                    k = (b * NKV + g) * 2 + qh
                    gate(o_ps, k + 1)
                    gate(o_lo, k + 1)
                    v.reciprocal(rden[:], ps[:, 5, :]).then_inc(o_rd, 1)
                    gate(o_rd, k + 1)
                    v.tensor_tensor(attn[:, qh, :], ps[:, 4, :], rden[:], ALU.mult).then_inc(o_nm, 1)

                def group(g, u, first=False, last=False):
                    for n in range(NSTEP):
                        if not last:
                            for k in pieces_of(n):
                                maximum(g + 1, 1 - u, k)
                            if n == NSTEP - 1:
                                minus_max(g + 1, 1 - u)
                        if n == 1 and not first:
                            normalise_attn(g - 1, 1)
                        if n == 3 + LAG:
                            normalise_attn(g, 0)

                for k in range(NPIECE):
                    maximum(0, 0, k)
                minus_max(0, 0)
                group(0, 0, first=True)
                with dve.Fori(0, 3) as gg:
                    group(gg * 2 + 1, 1)
                    group(gg * 2 + 2, 0)
                group(7, 1, last=True)
                normalise_attn(7, 1)

                with dve.Fori(0, 4) as n:
                    for t in range(T):
                        cols = h[:, t, bass.ds(n * 256, 256)]
                        gate(op_ps, (b * 4 + n) * T + t + 1)
                        v.tensor_tensor(cols, ps[:, t, 0:256], cols, ALU.add).then_inc(op_set, 1)
                gate(op_set, (b + 1) * 32 + 8)
                layernorm(b, 1)
                for pp in range(FH // 2):
                    u = pp % 2
                    if pp >= 2:
                        gate(z_out[u], (b * (FH // 4) + pp // 2) * 16)
                    gate(dn_ps, b * (FH // 2) + pp + 1)
                    v.tensor_copy(d_out[:, u, :], ps[:, 4 + 2 * u:6 + 2 * u, :].rearrange("p a n -> p (a n)")).then_inc(dn_set, 1)
                with dve.Fori(0, T // 2) as tt:
                    for u in range(2):
                        row = h[:, bass.ds(tt * 2 + u, 1), :].rearrange("p o n -> p (o n)")
                        gate(f_ps, b * T + tt * 2 + u + 1)
                        v.tensor_tensor(row, ps[:, 2 * u:2 * u + 2, :].rearrange("p a n -> p (a n)"), row, ALU.add).then_inc(f_set, 1)
                gate(stored, (b + 1) * (16 * T))

        @block.tensor
        def _(pe):
            mm_ = nc.tensor.matmul

            def gate(s, value):
                pe.wait_ge(s, value)
                pe.sem_inc(gate_pe, 1)

            pe.wait_ge(consts, 5)

            def halves(lhs_hi, lhs_lo, rhs_hi, rhs_lo):
                return ((lhs_hi, rhs_hi), (lhs_lo, rhs_hi), (lhs_hi, rhs_lo))

            def layernorm(ln):
                with pe.Fori(0, T // 2) as tt:
                    for u in range(2):
                        n = ln * T + tt * 2 + u
                        pe.wait_ge(y_set, n + 1)
                        pe.wait_ge(y_lo, n + 1)
                        for k in range(KT):
                            last = nc.tensor.transpose(ps[:, 4 + 2 * u + k // 4, P * (k % 4):P * (k % 4) + P], y[:, u, P * k:P * k + P], ident[:])
                        last.then_inc(y_ps, 1)

            with pe.Fori(0, B) as b:
                gate(w_lo, b * NCHUNK + 4 + 2)
                with pe.Fori(0, T // 2) as tt:
                    for u in range(2):
                        n = b * T + tt * 2 + u
                        pe.wait_ge(gathered[u], (b * (T // 2) + tt + 1) * 48)
                        for k in range(3):
                            last = nc.tensor.transpose(ps[:, u, R * k:R * k + R], a_rows[:, u, R * k:R * k + R], ident[:])
                        last.then_inc(at_ps, 1)
                        pe.wait_ge(at_lo, n + 1)
                        pe.wait_ge(h_set, n + 1)
                        for c in range(4):
                            dst = ps[:, 2 + 2 * u + c // 2, 256 * (c % 2):256 * (c % 2) + 256]
                            terms = [(l, r) for k in range(3) for l, r in halves(
                                a_t[:, u, 0, R * k:R * k + R], a_t[:, u, 1, R * k:R * k + R],
                                hi(c)[:, 256 * k:256 * k + 256], lo(c)[:, 256 * k:256 * k + 256])]
                            for k, (l, r) in enumerate(terms):
                                last = mm_(dst, l, r, start=k == 0, stop=k == len(terms) - 1)
                        last.then_inc(emb_ps, 1)
                layernorm(b * 2)
                pe.wait_ge(y_lo, (b * 2 + 1) * T + 2)
                pe.wait_ge(h_set, (b + 1) * T + 2)
                pe.wait_ge(w_lo, b * NCHUNK + 6 + 2)
                for t in range(T):
                    pe.wait_ge(v_set, b * T + t + 1)
                    terms = [(l, r) for k in range(KT) for l, r in halves(
                        x_hi[:, k, P * t:P * t + P], x_lo[:, k, P * t:P * t + P],
                        hi(k // 4)[:, 256 * (k % 4):256 * (k % 4) + 256], lo(k // 4)[:, 256 * (k % 4):256 * (k % 4) + 256])]
                    for k, (l, r) in enumerate(terms):
                        last = mm_(ps[:, t % 4, 0:256], l, r, start=k == 0, stop=k == len(terms) - 1)
                    last.then_inc(v_ps, 1)
                with pe.Fori(0, MT // 2) as mm:
                    for u in range(2):
                        pe.wait_ge(w_lo, b * NCHUNK + C_M + mm * 2 + u + 1 + 2)
                        for hf in range(2):
                            r = (b * MT + mm * 2 + u) * 2 + hf
                            pe.wait_ge(p_lo, r + 1)
                            terms = [(l, rr) for k in range(KT) for l, rr in halves(
                                hi(2 + u)[:, P * k:P * k + P], lo(2 + u)[:, P * k:P * k + P],
                                x_hi[:, k, H * hf:H * hf + H], x_lo[:, k, H * hf:H * hf + H])]
                            for k, (l, rr) in enumerate(terms):
                                last = mm_(ps[:, 4 + 2 * u + hf, :], l, rr, start=k == 0, stop=k == len(terms) - 1)
                            last.then_inc(p_ps, 1)
                pe.wait_ge(p_sin, (b + 1) * (2 * MT))
                pe.wait_ge(v_set, (b + 1) * T + 4)
                gate(k_ones, b + 1)

                def maximum(g, u, k, half):
                    gi = b * NKV + g
                    qt, kh, jp = PIECES[k]
                    w = min(P * (qt + 1) - H * kh, H)
                    if k == 0:
                        pe.wait_ge(qk_in[u], (b * (NKV // 2) + half + 1) * 96)
                        pe.wait_ge(m_row, gi + 1)
                    pe.wait_ge(mx_rd, gi * NPIECE + k + 1)
                    for x in range(2):
                        j = 2 * jp + x
                        last = mm_(ps[:, 6 + x, 0:w], ring[0:96, 4 * u + j, P * qt:P * qt + P], kst[0:96, u, H * kh:H * kh + w], start=True, stop=True)
                    last.then_inc(mx_ps, 1)

                def minus_max(g, u):
                    gi = b * NKV + g
                    pe.wait_ge(m_neg, gi + 1)
                    nc.tensor.transpose(ps[0:GQ * T, 6, 0:P], negm[:, u, :], ident[:]).then_inc(m_ps, 1)

                def scores(g, u, n):
                    gi = b * NKV + g
                    kt = STEPS[n][1]
                    q0, w = step_range(n)
                    if n == 0:
                        pe.wait_ge(m_in, (gi + 1) * 32)
                    pe.wait_ge(e_set, gi * NSTEP + n + 1)
                    for j in range(GQ):
                        last = mm_(ps[:, j, 0:w], kst[0:98, u, P * kt:P * kt + P], ring[0:98, 4 * u + j, q0:q0 + w], start=True, stop=True)
                    last.then_inc(st_ps, 1)

                def weighted(g, u, n):
                    gi = b * NKV + g
                    qh, kt = STEPS[n]
                    q0, w = step_range(n)
                    c0 = q0 - H * qh
                    if n == 0:
                        pe.wait_ge(vg_set, gi + 1)
                    if kt == 0:
                        pe.wait_ge(o_nm, gi * 2 + qh + 1)
                    pe.wait_ge(e_set, gi * NSTEP + n + 2)
                    if n in DIAG:
                        pe.wait_ge(e_mask, gi * len(DIAG) + DIAG.index(n) + 1)
                    for bank, lhs in ((4, vg[:, u, kt, :]), (5, ones[:])):
                        for j in range(GQ):
                            last = mm_(ps[HD * j:HD * j + HD, bank, c0:c0 + w], lhs, work[:, n % 3, j, 0:w],
                                       start=kt == 0, stop=kt == 4 * qh + 3, skip_group_check=True)
                    if kt == 4 * qh + 3:
                        last.then_inc(o_ps, 1)

                def group(g, u, half, first=False, last=False):
                    for n in range(NSTEP):
                        todo = [] if last else pieces_of(n)
                        if todo:
                            maximum(g + 1, 1 - u, todo.pop(0), half)
                        scores(g, u, n)
                        if todo:
                            maximum(g + 1, 1 - u, todo.pop(0), half)
                        if n >= LAG:
                            weighted(g, u, n - LAG)
                        elif not first:
                            weighted(g - 1, 1 - u, NSTEP + n - LAG)
                        if todo:
                            maximum(g + 1, 1 - u, todo.pop(0), half)
                    if not last:
                        minus_max(g + 1, 1 - u)

                for k in range(NPIECE):
                    maximum(0, 0, k, 0)
                minus_max(0, 0)
                group(0, 0, 0, first=True)
                with pe.Fori(0, 3) as gg:
                    group(gg * 2 + 1, 1, gg + 1)
                    group(gg * 2 + 2, 0, gg + 1)
                group(7, 1, 4, last=True)
                for n in range(NSTEP - LAG, NSTEP):
                    weighted(7, 1, n)

                gate(o_lo, (b + 1) * (2 * NKV) + 2)
                with pe.Fori(0, 2) as nn:
                    for nu in range(2):
                        n = nn * 2 + nu
                        pe.wait_ge(w_lo, b * NCHUNK + C_O + n * 2 + 2 + 2)
                        for t in range(T):
                            pe.wait_ge(op_set, (b * 4 + n) * T + t + 1)
                            terms = [(l, r) for k in range(KT) for l, r in halves(
                                x_hi[:, k, P * t:P * t + P], x_lo[:, k, P * t:P * t + P],
                                hi(2 * nu + k // 4)[:, 256 * (k % 4):256 * (k % 4) + 256],
                                lo(2 * nu + k // 4)[:, 256 * (k % 4):256 * (k % 4) + 256])]
                            for k, (l, r) in enumerate(terms):
                                last = mm_(ps[:, t, 0:256], l, r, start=k == 0, stop=k == len(terms) - 1)
                            last.then_inc(op_ps, 1)
                gate(op_set, (b + 1) * 32 + 8)
                layernorm(b * 2 + 1)
                pe.wait_ge(y_lo, (b * 2 + 2) * T + 2)
                pe.wait_ge(down_in, (b + 1) * 16)
                pe.wait_ge(w_lo, b * NCHUNK + NCHUNK + 2)
                for pp in range(FH // 2):
                    for e in range(2):
                        hh = 2 * pp + e
                        pe.wait_ge(t_in[e], (b * (FH // 2) + pp + 1) * 16)
                        for hf in range(2):
                            pe.wait_ge(gel_set, b * (2 * FH) + 2 * hh + hf + 1)
                            for m in range(2):
                                w0 = FM * (hh % 4) + P * m
                                for k, w in enumerate((hi(hh // 4), lo(hh // 4))):
                                    last = mm_(ps[:, 2 * hf + m, :], w[:, w0:w0 + P], kst[:, e, H * hf:H * hf + H], start=k == 0, stop=k == 1)
                            last.then_inc(up_ps, 1)
                    pe.wait_ge(dn_set, b * (FH // 2) + pp + 1)
                    pe.wait_ge(gel_set, b * (2 * FH) + 4 * pp + 4 + 2)
                    for hf in range(2):
                        for m in range(2):
                            for e in range(2):
                                w0 = ((2 * pp + e) * 2 + m) * FD
                                last = mm_(ps[FD * e:FD * e + FD, 4 + 2 * (pp % 2) + hf, :], down_sb[:, w0:w0 + FD],
                                           gel[:, 2 * e + hf, m, :], start=m == 0, stop=m == 1, skip_group_check=True)
                    last.then_inc(dn_ps, 1)
                pe.wait_ge(z_in, (b + 1) * 16)
                for t in range(T):
                    pe.wait_ge(f_set, b * T + t + 1)
                    for k in range(KT):
                        last = nc.tensor.transpose(ps[:, 2 * (t % 2) + k // 4, P * (k % 4):P * (k % 4) + P], z_sb[:, k, P * t:P * t + P], ident[:])
                    last.then_inc(f_ps, 1)


def _tiles(w, rows):
    k, n = w.shape[0] // P, w.shape[1] // rows
    return w.reshape(k, P, n, rows).transpose(2, 1, 0, 3).reshape(n, P, k * rows)


def kernel(**inputs):
    import numpy as np
    import concourse.bacc as bacc
    from concourse.bass_utils import run_bass_kernel_spmd as run

    a = {k: np.asarray(v) for k, v in inputs.items()}

    def columns(x):
        return np.ascontiguousarray(x.reshape(B * T, P).T)

    pairs = np.arange(HD).reshape(2, HD // 2).T.reshape(-1)

    def paired(w):
        return w.reshape(-1, HD, D)[:, pairs, :].reshape(-1, D)

    lora_b = np.stack([a["L0_tok_lora_B_cl"], a["L0_tok_lora_B_lm"], a["L0_tok_lora_B_cl_prime"]], 1)
    b_chunks = np.zeros((4, P, 1024), np.float32)
    b_chunks[:, :, 0:768] = lora_b.reshape(R, 3, 4, 256).transpose(2, 0, 1, 3).reshape(4, R, 768)
    wv = a["L0_attn_Wv"].T.reshape(2, 4, P, 256).transpose(0, 2, 1, 3).reshape(2, P, 1024)
    wk = _tiles(paired(a["L0_attn_Wk"]).T, P)
    wq = _tiles(paired(a["L0_attn_Wq"]).T, P)
    wo = a["L0_attn_Wo"].T.reshape(2, 4, P, 4, 256).transpose(3, 0, 2, 1, 4).reshape(8, P, 1024)
    up = a["L0_ffn_up"].reshape(4, 4, FD, FM).transpose(0, 2, 1, 3).reshape(4, FD, 4 * FM)
    up = np.concatenate([up, up], 1)
    chunks = np.concatenate([b_chunks, wv, wk, wq, wo, up], 0)
    down = a["L0_ffn_down"].reshape(FH, 2, P, FD).transpose(2, 0, 1, 3).reshape(P, FH * 2 * FD)

    inv = (np.float32(1.0) / np.float32(10000.0) ** (np.arange(0, HD, 2, dtype=np.float32) / np.float32(HD))).astype(np.float32)
    ang = np.outer(np.arange(S, dtype=np.float32), inv).astype(np.float32)
    cos = np.tile(np.repeat(np.cos(ang).T, 2, 0), (4, 1)).astype(np.float32)
    sin = (np.tile(np.repeat(np.sin(ang).T, 2, 0), (4, 1)) * np.tile(np.array([[1.0], [-1.0]]), (64, 1))).astype(np.float32)

    perm = a["L0_ffn_perm"].astype(np.int32) if a["L0_ffn_perm"].dtype != np.int32 else a["L0_ffn_perm"]
    perm_up = np.tile(perm.reshape(FH, FD), (1, 2)).T
    perm_down = perm.reshape(FH // 2, P).T
    arrays = {
        "ids": columns(a["x"]), "mask1": columns(a["mask_BS_i1_0"]), "mask0": columns(a["mask_BS_i0_1"]),
        "table_w": a["L0_tok_weight"], "table_a1": a["L0_tok_lora_A_cl"],
        "table_a23": np.concatenate([a["L0_tok_lora_A_lm"], a["L0_tok_lora_A_cl_prime"]], 1),
        "chunks": chunks, "down": down, "cos": cos, "sin": sin, "perm_up": perm_up, "perm_down": perm_down,
    }
    nc = bacc.Bacc("TRN2", target_bir_lowering=False, num_devices=1)
    feeds, aps = {}, []
    for name, arr in arrays.items():
        arr = np.ascontiguousarray(arr)
        feeds[f"{name}_dram"] = arr
        aps.append(nc.dram_tensor(f"{name}_dram", arr.shape, mybir.dt.from_np(arr.dtype), kind="ExternalInput").ap())
    out = nc.dram_tensor("out_dram", (B * S, D), F32, kind="ExternalOutput").ap()
    program(nc, *aps, out)
    r = run(nc, [feeds], core_ids=[0])
    return r.results[0]["out_dram"].reshape(B, S, D)
```

```python
import concourse.bass as bass
from concourse import mybir
from contextlib import ExitStack

F32 = mybir.dt.float32
F32R = mybir.dt.float32r
I32 = mybir.dt.int32
ALU = mybir.AluOpType
ACT = mybir.ActivationFunctionType
AX_X = mybir.AxisListType.X

P = 128
B, S, D = 4, 1024, 1024
V, R = 8000, 128
NH, NKV = 32, 8
HD = D // NH
GQ = NH // NKV
T = S // P
KT = D // P
H = S // 2
FH, FD, FM = 16, 64, 256
MT = 2 + NKV
SCALE = float(HD) ** -0.5
EPS = 1e-5
NEG = -3.0e38

C_B, C_V, C_M, C_O, C_U, NCHUNK = 0, 4, 6, 16, 24, 28
STEPS = [(qh, kt) for qh in range(2) for kt in range(4 * (qh + 1))]
NSTEP = len(STEPS)
DIAG = [n for n, (qh, kt) in enumerate(STEPS) if kt >= 4 * qh]
PIECES = [(qt, kh, j) for qt in range(T) for kh in range(qt // 4 + 1) for j in range(GQ)]
NPIECE = len(PIECES)
FIRST = 4 * GQ
USES = [("P", k) for k in range(FIRST + 2)] + [("T", 0)] + [("P", k) for k in range(FIRST + 2, NPIECE)] + [("T", 1)]
NUSE = len(USES)
SPREAD = [6, 4, 3, 2, 5, 5, 5, 5, 5, 4, 3, 3]
START = [[], []] + [list(range(NUSE * n // 6, NUSE * (n + 1) // 6)) for n in range(6)]
LAG = 2


def step_range(n):
    qh, kt = STEPS[n]
    q0 = max(H * qh, P * kt)
    return q0, H * (qh + 1) - q0


def uses_of(n):
    first = sum(SPREAD[:n])
    return list(range(first, first + SPREAD[n]))


def piece_width(k):
    qt, kh, _ = PIECES[k]
    return min(P * (qt + 1) - H * kh, H)


def shares(items, n):
    return [items[len(items) * k // n:len(items) * (k + 1) // n] for k in range(n)]


def program(nc, ids, mask1, mask0, table_w, table_a1, table_a23, chunks, down, cos, sin, perm_up, perm_down, out):
    with ExitStack() as ctx:
        def sb(name, shape, dt=F32):
            return ctx.enter_context(nc.sbuf_tensor(name, shape, dt))

        def sem(name):
            return ctx.enter_context(nc.semaphore(name))

        qk_dram = nc.dram_tensor("qk_dram", (2, MT * P, S), F32, kind="Internal").ap()
        y_dram = nc.dram_tensor("y_dram", (2 * D, S), F32, kind="Internal").ap()
        z_dram = nc.dram_tensor("z_dram", (D, S), F32, kind="Internal").ap()
        m_dram = nc.dram_tensor("m_dram", (2, 2, 2, FIRST, P), F32, kind="Internal").ap()

        h = sb("h", [P, T, D])
        x_hi = sb("x_hi", [P, KT, S], F32R)
        x_lo = sb("x_lo", [P, KT, S], F32R)
        ring = sb("ring", [P, 8, 1024], F32R)
        kst = sb("kst", [P, 2, S], F32R)
        work = sb("work", [P, 3, GQ, H])
        v_all = sb("v_all", [P, T, NKV * HD])
        vg = sb("vg", [P, 2, T, HD])
        raw = sb("raw", [P, 2, 1024])
        cos_sb = sb("cos_sb", [P, S])
        sin_sb = sb("sin_sb", [P, S])
        a_rows = sb("a_rows", [P, 2, 3 * R])
        attn = sb("attn", [P, 2, H])
        rden = sb("rden", [P, H // HD, HD])
        rcol = sb("rcol", [P, H // HD, 1])
        r_hi = sb("r_hi", [P, 2, H], F32R)
        ident = sb("ident", [P, P])
        causal = sb("causal", [P, P])
        ones = sb("ones", [P, HD])
        stats = sb("stats", [P, T, 2, 6])
        mv = sb("mv", [P, T, 2])
        ve = sb("ve", [P, T])
        sd = sb("sd", [P, T])
        rstd = sb("rstd", [P, T])
        nwt = sb("nwt", [P, T])
        mx = sb("mx", [P, 2, GQ, T, 3])
        negm = sb("negm", [P, 2, 2, FIRST])
        m_hi = sb("m_hi", [FIRST, 2, P], F32R)
        m_lo = sb("m_lo", [FIRST, 2, P], F32R)
        idx_raw = sb("idx_raw", [P, 3, B * T], I32)
        idx_neg = sb("idx_neg", [P, 3, B * T], I32)
        idx_all = sb("idx_all", [P, B * T, 3], I32)
        idx_now = sb("idx_now", [P, 2, 3], I32)
        pu = sb("pu", [P, FH], I32)
        pu_now = sb("pu_now", [P, 2, 1], I32)
        pd = sb("pd", [P, FH // 2], I32)
        pd_now = sb("pd_now", [P, 2, 1], I32)
        ps = ctx.enter_context(nc.psum_tensor("ps", [P, 8, 512], F32))

        r_lo = attn[:].bitcast(F32R)
        flat = work[:].rearrange("p a j n -> p (a j n)")
        w_rows = flat[:, 0:2048].rearrange("p (u n) -> p u n", u=2)
        y = flat[:, 2048:4096].rearrange("p (u n) -> p u n", u=2)
        r_cos = flat[:, 0:1024].rearrange("p (u n) -> p u n", u=2)
        r_sin = flat[:, 1024:2048].rearrange("p (u n) -> p u n", u=2)
        r_swap = flat[:, 2048:3072].rearrange("p (u n) -> p u n", u=2)
        gel = flat[:, 0:4096].rearrange("p (a m n) -> p a m n", a=4, m=2)
        d_out = flat[:, 4096:6144].rearrange("p (u n) -> p u n", u=2)
        kflat = kst[:].rearrange("p u n -> p (u n)")
        a_t = kflat[:, 0:1536].rearrange("p (u x n) -> p u x n", u=2, x=2)
        down_sb = v_all[:].rearrange("p t n -> p (t n)")
        z_sb = x_hi[:].bitcast(F32)

        def hi(s):
            return ring[:, 2 * s, :]

        def lo(s):
            return ring[:, 2 * s + 1, :]

        def f32(ap):
            return ap.bitcast(F32)

        loaded = sem("loaded")
        consts = sem("consts")
        idx_ok = sem("idx_ok")
        prep = sem("prep")
        raw_in = [sem(f"raw_in{u}") for u in range(2)]
        w_hi = sem("w_hi")
        w_lo = sem("w_lo")
        idx_cp = sem("idx_cp")
        gathered = [sem(f"gathered{u}") for u in range(2)]
        at_ps = sem("at_ps")
        at_hi = sem("at_hi")
        at_lo = sem("at_lo")
        emb_ps = sem("emb_ps")
        h_set = sem("h_set")
        st_set = sem("st_set")
        mv_set = sem("mv_set")
        ln_ve = sem("ln_ve")
        ln_sd = sem("ln_sd")
        ln_nw = sem("ln_nw")
        y_set = sem("y_set")
        y_ps = sem("y_ps")
        y_hi = sem("y_hi")
        y_lo = sem("y_lo")
        v_ps = sem("v_ps")
        v_set = sem("v_set")
        p_ps = sem("p_ps")
        p_cos = sem("p_cos")
        p_sin = sem("p_sin")
        p_swap = sem("p_swap")
        p_add = sem("p_add")
        p_hi = sem("p_hi")
        p_lo = sem("p_lo")
        p_out = [sem(f"p_out{u}") for u in range(2)]
        k_ones = sem("k_ones")
        qk_in = [[sem(f"qk_in{u}{x}") for x in range(2)] for u in range(2)]
        mx_ps = sem("mx_ps")
        mx_rd = sem("mx_rd")
        m_neg = sem("m_neg")
        m_ps = sem("m_ps")
        m_h = sem("m_h")
        m_st = sem("m_st")
        m_in = [sem(f"m_in{x}") for x in range(2)]
        st_ps = sem("st_ps")
        e_set = sem("e_set")
        e_mask = sem("e_mask")
        vg_set = sem("vg_set")
        o_ps = sem("o_ps")
        o_rd = sem("o_rd")
        o_nm = sem("o_nm")
        o_hi = sem("o_hi")
        o_lo = sem("o_lo")
        op_ps = sem("op_ps")
        op_set = sem("op_set")
        y_out = sem("y_out")
        down_in = sem("down_in")
        pu_cp = sem("pu_cp")
        t_in = [sem(f"t_in{u}") for u in range(2)]
        up_ps = sem("up_ps")
        gel_set = sem("gel_set")
        dn_ps = sem("dn_ps")
        dn_set = sem("dn_set")
        pd_cp = sem("pd_cp")
        z_out = [sem(f"z_out{u}") for u in range(2)]
        z_in = [sem(f"z_in{x}") for x in range(4)]
        f_ps = sem("f_ps")
        f_set = sem("f_set")
        stored = sem("stored")
        gate_pool = sem("gate_pool")
        gate_act = sem("gate_act")
        gate_dve = sem("gate_dve")
        gate_pe = sem("gate_pe")
        gate_sp = sem("gate_sp")

        block = ctx.enter_context(nc.Block())

        @block.sync
        def _(sp):
            def gate(s, value):
                sp.wait_ge(s, value)
                sp.sem_inc(gate_sp, 1)

            for dst, src in ((idx_raw[:, 0, :], ids), (idx_raw[:, 1, :], mask1), (idx_raw[:, 2, :], mask0),
                             (cos_sb[:], cos), (sin_sb[:], sin), (pu[:], perm_up), (pd[:], perm_down)):
                sp.dma_start(dst, src).then_inc(loaded, 16)

            def load_chunk(b, c, u):
                gate(w_lo, b * NCHUNK + c + 1)
                sp.dma_start(raw[:, u, :], chunks[bass.ds(c, 1), :, :].rearrange("o p n -> (o p) n")).then_inc(raw_in[u], 16)

            def load_group(b, g, u, x):
                cols = slice(H * x, H * x + H)
                for row, half in ((0, 0), (1, 1), (2, 0)):
                    sp.dma_start(f32(ring[HD * row:HD * row + HD, 4 * u:4 * u + GQ, cols]),
                                 qk_dram[half, bass.ds((2 + g) * P, P), cols].rearrange("(j d) n -> d j n", d=HD)).then_inc(qk_in[u][x], 16)
                for row, half in ((0, 0), (1, 0), (2, 1)):
                    sp.dma_start(f32(kst[HD * row:HD * row + HD, u, cols]),
                                 qk_dram[half, bass.ds(g * HD, HD), cols]).then_inc(qk_in[u][x], 16)

            def max_rows(gi, u, x):
                gate(mx_rd, gi * NUSE + USES.index(("T", x)) + 3)
                sp.dma_start(m_dram[0, u, x, :, :], f32(m_hi[:, x, :])).then_inc(m_st, 16)
                sp.dma_start(m_dram[1, u, x, :, :], f32(m_lo[:, x, :])).then_inc(m_st, 16)
                gate(m_st, (gi * 2 + x + 1) * 32)
                for half in range(2):
                    sp.dma_start(f32(ring[96 + half:97 + half, 4 * u:4 * u + GQ, H * x:H * x + H]),
                                 m_dram[half, u, x, :, :].rearrange("(o j t) n -> o j (t n)", o=1, j=GQ)).then_inc(m_in[x], 16)

            with sp.Fori(0, B) as b:
                for c in range(6):
                    load_chunk(b, c, c % 2)
                for c in range(6, 10):
                    load_chunk(b, c, c % 2)
                def store(m):
                    for hf in range(2):
                        gate(p_lo, (b * MT + m) * 2 + hf + 3)
                        for x, src in ((0, r_hi), (1, r_lo)):
                            sp.dma_start(qk_dram[x, bass.ds(m * P, P), H * hf:H * hf + H], f32(src[:, hf, :])).then_inc(p_out[hf], 16)

                with sp.Fori(0, 3) as mm:
                    for u in range(2):
                        store(mm * 2 + u)
                        load_chunk(b, mm * 2 + u + 10, u)
                for hf in range(2):
                    gate(p_out[hf], (b * MT + 6) * 32 + 32)
                for x in range(2):
                    load_group(b, 0, 0, x)
                for m in range(6, MT):
                    store(m)
                    if m < 8:
                        load_chunk(b, m + 10, m % 2)
                    if m == 8:
                        max_rows(b * NKV, 0, 0)
                for hf in range(2):
                    gate(p_out[hf], (b + 1) * (MT * 32) + 32)
                for x in range(2):
                    load_group(b, 1, 1, x)
                max_rows(b * NKV, 0, 1)

                def group(g, u, ahead=True):
                    gi = b * NKV + g
                    max_rows(gi + 1, 1 - u, 0)
                    if ahead:
                        gate(st_ps, gi * NSTEP + 8)
                        load_group(b, g + 2, u, 0)
                        gate(st_ps, gi * NSTEP + NSTEP)
                        load_group(b, g + 2, u, 1)
                    max_rows(gi + 1, 1 - u, 1)

                with sp.Fori(0, 3) as gg:
                    for u in range(2):
                        group(gg * 2 + u, u)
                group(6, 0, ahead=False)
                gate(o_ps, (b + 1) * (2 * NKV))
                sp.dma_start(down_sb, down).then_inc(down_in, 16)
                for c in range(18, 20):
                    load_chunk(b, c, c % 2)
                with sp.Fori(0, 4) as n:
                    for u in range(2):
                        load_chunk(b, n * 2 + u + 20, u)
                with sp.Fori(0, T) as t:
                    gate(y_lo, (b * 2 + 1) * T + t + 3)
                    for x, src in enumerate((x_hi, x_lo)):
                        sp.dma_start(y_dram[D * x:D * x + D, bass.ds(t * P, P)].rearrange("(k p) n -> p k n", p=P),
                                     f32(src[:, :, bass.ds(t * P, P)])).then_inc(y_out, 16)
                gate(y_out, (b + 1) * (32 * T))
                for u in range(2):
                    gate(z_out[u], (b + 1) * (16 * FH // 4))
                for x in range(4):
                    cols = slice(2 * P * x, 2 * P * x + 2 * P)
                    sp.dma_start(z_sb[:, :, cols], z_dram[:, cols].rearrange("(k p) n -> p k n", p=P)).then_inc(z_in[x], 16)
                with sp.Fori(0, T) as t:
                    gate(f_set, b * T + t + 3)
                    sp.dma_start(out[bass.ds((b * T + t) * P, P), :],
                                 h[:, bass.ds(t, 1), :].rearrange("p o n -> p (o n)")).then_inc(stored, 16)
            sp.wait_ge(stored, 16 * B * T)

        @block.gpsimd
        def _(pool):
            pool.sem_inc(w_lo, 2)
            pool.sem_inc(p_lo, 2)
            pool.sem_inc(o_lo, 2)
            pool.memset(ident[:], 0.0).then_inc(consts, 1)
            pool.memset(causal[:], 0.0).then_inc(consts, 1)
            pool.memset(ones[:], 1.0).then_inc(consts, 1)
            pool.wait_ge(consts, 3)
            pool.affine_select(out=ident[:], in_=ident[:], compare_op=ALU.not_equal, fill=1.0, base=0,
                               pattern=[[-1, P]], channel_multiplier=1).then_inc(consts, 1)
            pool.affine_select(out=causal[:], in_=causal[:], compare_op=ALU.is_ge, fill=NEG, base=0,
                               pattern=[[-1, P]], channel_multiplier=1).then_inc(consts, 1)
            pool.wait_ge(idx_ok, 1)

            def gate(s, value):
                pool.wait_ge(s, value)
                pool.sem_inc(gate_pool, 1)

            def split_lo(b, c, s, u):
                gate(w_hi, b * NCHUNK + c + 1)
                pool.tensor_tensor(lo(s), raw[:, u, :], f32(hi(s)), ALU.subtract).then_inc(w_lo, 1)

            with pool.Fori(0, B) as b:
                for c in range(4):
                    split_lo(b, C_B + c, c, c % 2)
                with pool.Fori(0, T // 2) as tt:
                    for u in range(2):
                        n = b * T + tt * 2 + u
                        gate(h_set, n + 1)
                        pool.tensor_copy(idx_now[:, u, :], idx_all[:, bass.ds(n, 1), :].rearrange("p o i -> p (o i)")).then_inc(idx_cp, 1)
                        gate(idx_cp, n + 1)
                        for k, (dst, table, rows) in enumerate(((w_rows[:, u, :], table_w, V), (a_rows[:, u, 0:R], table_a1, V),
                                                               (a_rows[:, u, R:3 * R], table_a23, V))):
                            pool.indirect_dma_start(dst, None, table, bass.IndirectOffsetOnAxis(ap=idx_now[:, u, k:k + 1], axis=0)).then_inc(gathered[u], 16)
                for c, s in ((4, 0), (5, 1), (6, 2), (7, 3)):
                    split_lo(b, c, s, c % 2)

                gate(emb_ps, (b + 1) * T)
                gate(w_lo, b * NCHUNK + 8 + 2)
                pool.memset(f32(kst[96:98, :, :]), 1.0).then_inc(k_ones, 1)
                gate(k_ones, b + 1)

                def rotated_lo(m, hf):
                    gate(p_hi, (b * MT + m) * 2 + hf + 1)
                    pool.tensor_tensor(r_lo[:, hf, :], r_cos[:, hf, :], f32(r_hi[:, hf, :]), ALU.subtract).then_inc(p_lo, 1)

                with pool.Fori(0, MT // 2 - 1) as mm:
                    for u in range(2):
                        rotated_lo(mm * 2 + u, 0)
                        split_lo(b, mm * 2 + u + 8, 2 + u, u)
                        rotated_lo(mm * 2 + u, 1)
                for u in range(2):
                    rotated_lo(MT - 2 + u, 0)
                    rotated_lo(MT - 2 + u, 1)

                def values(g, u):
                    pool.tensor_copy(vg[:, u, :, :], v_all[:, :, bass.ds(g * HD, HD)]).then_inc(vg_set, 1)

                def group(g, u, first=False, last=False):
                    gi = b * NKV + g
                    for n in range(NSTEP):
                        if n in DIAG:
                            gate(e_set, gi * NSTEP + n + 2)
                            pool.affine_select(out=work[:, n % 3, :, 0:P], in_=work[:, n % 3, :, 0:P], compare_op=ALU.is_ge,
                                               fill=0.0, base=0, pattern=[[0, GQ], [1, P]], channel_multiplier=-1).then_inc(e_mask, 1)
                        if n == 2 and not first:
                            split_attn(g - 1, 1)
                        if n == 3 and not last:
                            if not first:
                                gate(o_ps, gi * 2)
                            values(g + 1, 1 - u)
                        if n == 8:
                            split_attn(g, 0)

                def split_attn(g, qh):
                    k = (b * NKV + g) * 2 + qh
                    gate(o_hi, k + 1)
                    col = x_lo[:, bass.ds(g, 1), H * qh:H * qh + H].rearrange("p o n -> p (o n)")
                    src = x_hi[:, bass.ds(g, 1), H * qh:H * qh + H].rearrange("p o n -> p (o n)")
                    pool.tensor_tensor(col, attn[:, qh, :], f32(src), ALU.subtract).then_inc(o_lo, 1)

                gate(v_set, (b + 1) * T + 4)
                values(0, 0)
                group(0, 0, first=True)
                with pool.Fori(0, 3) as gg:
                    group(gg * 2 + 1, 1)
                    group(gg * 2 + 2, 0)
                group(7, 1, last=True)
                split_attn(7, 1)

                for c in range(16, 20):
                    split_lo(b, c, c - 16, c % 2)
                with pool.Fori(0, 2) as nn:
                    for k in range(4):
                        split_lo(b, nn * 4 + 20 + k, k, k % 2)
                gate(y_out, (b + 1) * (32 * T))

                def gather(hh, u):
                    pool.tensor_copy(pu_now[:, u, :], pu[:, bass.ds(hh, 1)]).then_inc(pu_cp, 1)
                    gate(pu_cp, b * FH + hh + 1)
                    pool.indirect_dma_start(f32(kst[:, u, :]), None, y_dram, bass.IndirectOffsetOnAxis(ap=pu_now[:, u, :], axis=0)).then_inc(t_in[u], 16)

                for u in range(2):
                    gather(u, u)
                for pp in range(FH // 2):
                    for u in range(2):
                        if pp < FH // 2 - 1:
                            gate(up_ps, b * (2 * FH) + (2 * pp + u) * 2 + 2)
                            gather(2 * pp + 2 + u, u)
                    gate(dn_set, b * (FH // 2) + pp + 3)
                    pool.tensor_copy(pd_now[:, pp % 2, :], pd[:, pp:pp + 1]).then_inc(pd_cp, 1)
                    gate(pd_cp, b * (FH // 2) + pp + 1)
                    pool.indirect_dma_start(z_dram, bass.IndirectOffsetOnAxis(ap=pd_now[:, pp % 2, :], axis=0),
                                            d_out[:, pp % 2, :], None).then_inc(z_out[pp % 2], 16)

        @block.scalar
        def _(act):
            act.sem_inc(v_set, 4)
            act.sem_inc(e_set, 1)
            act.sem_inc(gel_set, 2)

            def gate(s, value):
                act.wait_ge(s, value)
                act.sem_inc(gate_act, 1)

            def split_hi(b, pair, s, u):
                gate(raw_in[u], (b * (NCHUNK // 2) + pair + 1) * 16)
                act.activation(hi(s), raw[:, u, :], ACT.Copy).then_inc(w_hi, 1)

            def layernorm(b, which):
                act.wait_ge(ln_ve, b * 2 + which + 1)
                act.activation(sd[:], ve[:], ACT.Sqrt).then_inc(ln_sd, 1)
                with act.Fori(0, T // 2) as tt:
                    for u in range(2):
                        t = tt * 2 + u
                        gate(y_ps, (b * 2 + which) * T + t + 1)
                        act.activation(x_hi[:, :, bass.ds(t * P, P)],
                                       ps[:, 4 + 2 * u:6 + 2 * u, :].rearrange("p a (k n) -> p (a k) n", n=P), ACT.Copy).then_inc(y_hi, 1)

            with act.Fori(0, B) as b:
                for c in range(4):
                    split_hi(b, c // 2, c, c % 2)
                with act.Fori(0, T // 2) as tt:
                    for u in range(2):
                        act.wait_ge(at_ps, b * T + tt * 2 + u + 1)
                        act.activation(a_t[:, u, 0, :], ps[:, u, 0:3 * R], ACT.Copy).then_inc(at_hi, 1)
                act.wait_ge(emb_ps, (b + 1) * T)
                for c in range(4, 8):
                    split_hi(b, c // 2, c - 4, c % 2)
                layernorm(b, 0)
                for t in range(T):
                    act.wait_ge(v_ps, b * T + t + 1)
                    act.activation(v_all[:, t, :], ps[:, 4 + t % 4, 0:NKV * HD], ACT.Copy).then_inc(v_set, 1)

                def rotated_hi(m, hf):
                    gate(p_add, (b * MT + m) * 2 + hf + 1)
                    act.wait_ge(p_out[hf], (b * MT + m + 1) * 32)
                    act.activation(r_hi[:, hf, :], r_cos[:, hf, :], ACT.Copy).then_inc(p_hi, 1)

                with act.Fori(0, MT // 2 - 1) as mm:
                    for u in range(2):
                        rotated_hi(mm * 2 + u, 0)
                        gate(p_ps, (b * MT + mm * 2 + u + 1) * 2)
                        split_hi(b, mm + 4, 2 + u, u)
                        rotated_hi(mm * 2 + u, 1)
                for u in range(2):
                    rotated_hi(MT - 2 + u, 0)
                    rotated_hi(MT - 2 + u, 1)

                def group(g, first=False):
                    gi = b * NKV + g
                    for n in range(NSTEP):
                        w = step_range(n)[1]
                        act.wait_ge(st_ps, gi * NSTEP + n + 1)
                        act.activation(work[:, n % 3, :, 0:w], ps[:, 0:GQ, 0:w], ACT.Exp, scale=SCALE).then_inc(e_set, 1)
                        if n == 1 and not first:
                            attn_hi(g - 1, 1)
                        if n == 7:
                            attn_hi(g, 0)

                def attn_hi(g, qh):
                    gate(o_nm, (b * NKV + g) * 2 + qh + 2)
                    act.activation(x_hi[:, bass.ds(g, 1), H * qh:H * qh + H].rearrange("p o n -> p (o n)"),
                                   attn[:, qh, :], ACT.Copy).then_inc(o_hi, 1)

                group(0, first=True)
                with act.Fori(0, 3) as gg:
                    group(gg * 2 + 1)
                    group(gg * 2 + 2)
                group(7)
                attn_hi(7, 1)
                gate(st_ps, (b + 1) * (NKV * NSTEP))
                for c in range(16, 20):
                    split_hi(b, c // 2, c - 16, c % 2)
                with act.Fori(0, 2) as nn:
                    for k in range(4):
                        gate(op_ps, (b * 4 + nn * 2 + k // 2 + 1) * T)
                        split_hi(b, nn * 2 + 10 + k // 2, k, k % 2)
                layernorm(b, 1)
                for hh in range(FH):
                    for hf in range(2):
                        act.wait_ge(up_ps, b * (2 * FH) + 2 * hh + hf + 1)
                        if hh >= 2 and hf == 0:
                            act.wait_ge(dn_ps, b * (FH // 2) + hh // 2)
                        act.activation(gel[:, 2 * (hh % 2) + hf, :, :], ps[:, 2 * hf:2 * hf + 2, :], ACT.Gelu).then_inc(gel_set, 1)

        @block.vector
        def _(dve):
            v = nc.vector
            dve.sem_inc(h_set, 2)
            dve.sem_inc(y_lo, 2)
            dve.sem_inc(p_out[0], 32)
            dve.sem_inc(p_out[1], 32)
            dve.sem_inc(mx_rd, 2)
            dve.sem_inc(o_nm, 1)
            dve.sem_inc(op_set, 8)
            dve.sem_inc(dn_set, 2)
            dve.sem_inc(f_set, 2)

            def gate(s, value):
                dve.wait_ge(s, value)
                dve.sem_inc(gate_dve, 1)

            chain = [0]

            def link(ins):
                chain[0] += 1
                ins.then_inc(prep, 1)
                dve.wait_ge(prep, chain[0])

            dve.wait_ge(loaded, 7 * 16)
            link(v.memset(mx[:], NEG))
            link(v.tensor_tensor(idx_raw[:, 1, :], idx_raw[:, 1, :], idx_raw[:, 0, :], ALU.mult))
            link(v.tensor_tensor(idx_raw[:, 2, :], idx_raw[:, 2, :], idx_raw[:, 0, :], ALU.mult))
            link(v.tensor_scalar(idx_neg[:], idx_raw[:], 0, V, ALU.is_lt, ALU.mult))
            link(v.tensor_tensor(idx_raw[:], idx_raw[:], idx_neg[:], ALU.add))
            link(v.tensor_scalar(idx_all[:].rearrange("p n i -> p i n"), idx_raw[:], 0, V - 1, ALU.max, ALU.min))
            link(v.tensor_scalar(pu[FD:P, :], pu[FD:P, :], D, None, ALU.add))
            dve.wait_ge(consts, 5)
            dve.sem_inc(idx_ok, 1)

            def tile_stats(t):
                for k in range(2):
                    v.bn_stats(out=stats[:, bass.ds(t, 1), k, :].rearrange("p o n -> p (o n)"),
                               in_=h[:, bass.ds(t, 1), H * k:H * k + H].rearrange("p o n -> p (o n)")).then_inc(st_set, 1)

            def layernorm(b, which):
                ln = b * 2 + which
                gate(st_set, (ln + 1) * (2 * T))
                for t in range(T):
                    v.bn_aggr(out=mv[:, t, :], in_=stats[:, t, :, :].rearrange("p k s -> p (k s)")).then_inc(mv_set, 1)
                gate(mv_set, (ln + 1) * T)
                v.tensor_scalar(ve[:], mv[:, :, 1], EPS, None, ALU.add).then_inc(ln_ve, 1)
                gate(ln_sd, ln + 1)
                v.reciprocal(rstd[:], sd[:]).then_inc(ln_nw, 1)
                gate(ln_nw, ln * 5 + 1)
                v.tensor_tensor(nwt[:], rstd[:], rstd[:], ALU.mult).then_inc(ln_nw, 1)
                gate(ln_nw, ln * 5 + 2)
                v.tensor_tensor(nwt[:], nwt[:], ve[:], ALU.mult).then_inc(ln_nw, 1)
                gate(ln_nw, ln * 5 + 3)
                v.tensor_scalar(nwt[:], nwt[:], -0.5, 1.5, ALU.mult, ALU.add).then_inc(ln_nw, 1)
                gate(ln_nw, ln * 5 + 4)
                v.tensor_tensor(rstd[:], rstd[:], nwt[:], ALU.mult).then_inc(ln_nw, 1)
                gate(ln_nw, ln * 5 + 5)

                def normalise(t, u):
                    gate(y_lo, ln * T + t + 1)
                    v.tensor_scalar(y[:, u, :], h[:, bass.ds(t, 1), :].rearrange("p o n -> p (o n)"),
                                    mv[:, bass.ds(t, 1), 0:1].rearrange("p o n -> p (o n)"), rstd[:, bass.ds(t, 1)],
                                    ALU.subtract, ALU.mult).then_inc(y_set, 1)

                def split(t, u):
                    gate(y_hi, ln * T + t + 1)
                    cols = bass.ds(t * P, P)
                    v.tensor_tensor(x_lo[:, :, cols], ps[:, 4 + 2 * u:6 + 2 * u, :].rearrange("p a (k n) -> p (a k) n", n=P),
                                    f32(x_hi[:, :, cols]), ALU.subtract).then_inc(y_lo, 1)

                normalise(0, 0)
                normalise(1, 1)
                with dve.Fori(0, T // 2 - 1) as tt:
                    for u in range(2):
                        split(tt * 2 + u, u)
                        normalise(tt * 2 + u + 2, u)
                split(T - 2, 0)
                split(T - 1, 1)

            with dve.Fori(0, B) as b:
                with dve.Fori(0, T // 2) as tt:
                    for u in range(2):
                        n = b * T + tt * 2 + u
                        gate(at_hi, n + 1)
                        v.tensor_tensor(a_t[:, u, 1, :], ps[:, u, 0:3 * R], f32(a_t[:, u, 0, :]), ALU.subtract).then_inc(at_lo, 1)
                        gate(emb_ps, n + 1)
                        v.scalar_tensor_tensor(h[:, bass.ds(tt * 2 + u, 1), :].rearrange("p o n -> p (o n)"),
                                               ps[:, 2 + 2 * u:4 + 2 * u, :].rearrange("p a n -> p (a n)"), 2.0, w_rows[:, u, :],
                                               ALU.mult, ALU.add).then_inc(h_set, 1)
                        gate(h_set, n + 3)
                        tile_stats(tt * 2 + u)
                layernorm(b, 0)
                def rotate(m, u, hf):
                    r = (b * MT + m) * 2 + hf
                    gate(p_lo, r + 1)
                    gate(p_ps, r + 1)
                    bank = ps[:, 2 * u + hf, :]
                    v.tensor_tensor(r_sin[:, hf, :], bank, sin_sb[:, H * hf:H * hf + H], ALU.mult).then_inc(p_sin, 1)
                    v.tensor_tensor(r_cos[:, hf, :], bank, cos_sb[:, H * hf:H * hf + H], ALU.mult).then_inc(p_cos, 1)
                    gate(p_sin, r + 1)
                    v.stream_shuffle(r_swap[:, hf, :], r_sin[:, hf, :], [i ^ 1 for i in range(32)]).then_inc(p_swap, 1)
                    gate(p_cos, r + 1)
                    gate(p_swap, r + 1)
                    v.tensor_tensor(r_cos[:, hf, :], r_cos[:, hf, :], r_swap[:, hf, :], ALU.add).then_inc(p_add, 1)

                def maximum(g, u, k):
                    gi = b * NKV + g
                    bank = ps[:, 6 + k % 2, :]
                    kind, n = USES[k]
                    if kind == "P":
                        qt, kh, j = PIECES[n]
                        w = piece_width(n)
                        gate(mx_ps, gi * NPIECE + n + 1)
                        last = None
                        if kh == qt // 4:
                            w -= P
                            last = v.tensor_tensor_reduce(out=bank[:, w:w + P], in0=bank[:, w:w + P], in1=causal[:], scale=1.0, scalar=NEG,
                                                          op0=ALU.add, op1=ALU.max, accum_out=mx[:, u, j, qt, 2:3])
                        if w:
                            last = v.tensor_reduce(out=mx[:, u, j, qt, kh:kh + 1], in_=bank[:, 0:w], axis=AX_X, op=ALU.max)
                        last.then_inc(mx_rd, 1)
                        if n in (FIRST - 1, NPIECE - 1):
                            x = n // FIRST if n < FIRST else 1
                            gate(mx_rd, gi * NUSE + k + 3)
                            v.tensor_reduce(out=negm[:, u, x, :].rearrange("p (j t) -> p j t", j=GQ), in_=mx[:, u, :, 4 * x:4 * x + 4, :],
                                            axis=AX_X, op=ALU.max, negate=True).then_inc(m_neg, 1)
                    else:
                        gate(m_ps, gi * 2 + n + 1)
                        v.tensor_copy(m_hi[:, n, :], bank[0:FIRST, 0:P]).then_inc(m_h, 1)
                        gate(m_h, gi * 2 + n + 1)
                        v.tensor_tensor(m_lo[:, n, :], bank[0:FIRST, 0:P], f32(m_hi[:, n, :]), ALU.subtract).then_inc(mx_rd, 1)

                def normalise_attn(g, qh):
                    k = (b * NKV + g) * 2 + qh
                    gate(o_ps, k + 1)
                    gate(o_lo, k + 1)
                    v.transpose(rden[:].rearrange("p c i -> p (c i)"), ps[:, 5, :]).then_inc(o_rd, 1)
                    gate(o_rd, k * 3 + 1)
                    v.reciprocal(rcol[:], rden[:, :, 0:1]).then_inc(o_rd, 1)
                    gate(o_rd, k * 3 + 2)
                    v.transpose(rden[:], rcol[:].to_broadcast([P, H // HD, HD])).then_inc(o_rd, 1)
                    gate(o_rd, k * 3 + 3)
                    v.tensor_tensor(attn[:, qh, :], ps[:, 4, :], rden[:].rearrange("p c i -> p (c i)"), ALU.mult).then_inc(o_nm, 1)

                with dve.Fori(0, 3) as mm:
                    for u in range(2):
                        for hf in range(2):
                            rotate(mm * 2 + u, u, hf)
                for n in range(8):
                    for k in START[n]:
                        maximum(0, 0, k)
                    rotate(6 + n // 2, n // 2 % 2, n % 2)

                def group(g, u, first=False, last=False):
                    for n in range(NSTEP):
                        todo = [] if last else uses_of(n)
                        for k in todo[:2]:
                            maximum(g + 1, 1 - u, k)
                        if n == 1 and not first:
                            normalise_attn(g - 1, 1)
                        if n == 3 + LAG:
                            normalise_attn(g, 0)
                        for k in todo[2:]:
                            maximum(g + 1, 1 - u, k)

                group(0, 0, first=True)
                with dve.Fori(0, 3) as gg:
                    group(gg * 2 + 1, 1)
                    group(gg * 2 + 2, 0)
                group(7, 1, last=True)
                normalise_attn(7, 1)

                def add_output(n, t):
                    cols = h[:, t, bass.ds(n * 256, 256)]
                    gate(op_ps, (b * 4 + n) * T + t + 1)
                    v.tensor_tensor(cols, ps[:, t, 0:256], cols, ALU.add).then_inc(op_set, 1)

                with dve.Fori(0, 3) as n:
                    for t in range(T):
                        add_output(n, t)
                for t in range(T):
                    add_output(3, t)
                    gate(op_set, (b * 4 + 3) * T + t + 1 + 8)
                    tile_stats(t)
                layernorm(b, 1)
                for pp in range(FH // 2):
                    u = pp % 2
                    if pp >= 2:
                        gate(z_out[u], (b * (FH // 4) + pp // 2) * 16)
                    gate(dn_ps, b * (FH // 2) + pp + 1)
                    v.tensor_copy(d_out[:, u, :], ps[:, 4 + 2 * u:6 + 2 * u, :].rearrange("p a n -> p (a n)")).then_inc(dn_set, 1)
                with dve.Fori(0, T // 2) as tt:
                    for u in range(2):
                        row = h[:, bass.ds(tt * 2 + u, 1), :].rearrange("p o n -> p (o n)")
                        gate(f_ps, b * T + tt * 2 + u + 1)
                        v.tensor_tensor(row, ps[:, 2 * u:2 * u + 2, :].rearrange("p a n -> p (a n)"), row, ALU.add).then_inc(f_set, 1)
                gate(stored, (b + 1) * (16 * T))

        @block.tensor
        def _(pe):
            mm_ = nc.tensor.matmul

            def gate(s, value):
                pe.wait_ge(s, value)
                pe.sem_inc(gate_pe, 1)

            pe.wait_ge(consts, 5)

            def halves(lhs_hi, lhs_lo, rhs_hi, rhs_lo):
                return ((lhs_hi, rhs_hi), (lhs_lo, rhs_hi), (lhs_hi, rhs_lo))

            def layernorm(ln):
                with pe.Fori(0, T // 2) as tt:
                    for u in range(2):
                        n = ln * T + tt * 2 + u
                        pe.wait_ge(y_set, n + 1)
                        pe.wait_ge(y_lo, n + 1)
                        for k in range(KT):
                            last = nc.tensor.transpose(ps[:, 4 + 2 * u + k // 4, P * (k % 4):P * (k % 4) + P], y[:, u, P * k:P * k + P], ident[:])
                        last.then_inc(y_ps, 1)

            with pe.Fori(0, B) as b:
                gate(w_lo, b * NCHUNK + 4 + 2)
                def turn_rows(tt, u):
                    pe.wait_ge(gathered[u], (b * (T // 2) + tt + 1) * 48)
                    for k in range(3):
                        last = nc.tensor.transpose(ps[:, u, R * k:R * k + R], a_rows[:, u, R * k:R * k + R], ident[:])
                    last.then_inc(at_ps, 1)

                def embed(tt, u):
                    n = b * T + tt * 2 + u
                    pe.wait_ge(at_lo, n + 1)
                    pe.wait_ge(h_set, n + 1)
                    for c in range(4):
                        dst = ps[:, 2 + 2 * u + c // 2, 256 * (c % 2):256 * (c % 2) + 256]
                        terms = [(l, r) for k in range(3) for l, r in halves(
                            a_t[:, u, 0, R * k:R * k + R], a_t[:, u, 1, R * k:R * k + R],
                            hi(c)[:, 256 * k:256 * k + 256], lo(c)[:, 256 * k:256 * k + 256])]
                        for k, (l, r) in enumerate(terms):
                            last = mm_(dst, l, r, start=k == 0, stop=k == len(terms) - 1)
                    last.then_inc(emb_ps, 1)

                turn_rows(0, 0)
                with pe.Fori(0, T // 2 - 1) as tt:
                    turn_rows(tt, 1)
                    embed(tt, 0)
                    turn_rows(tt + 1, 0)
                    embed(tt, 1)
                turn_rows(T // 2 - 1, 1)
                embed(T // 2 - 1, 0)
                embed(T // 2 - 1, 1)
                layernorm(b * 2)
                pe.wait_ge(y_lo, (b * 2 + 1) * T + 2)
                pe.wait_ge(h_set, (b + 1) * T + 2)
                pe.wait_ge(w_lo, b * NCHUNK + 6 + 2)
                for t in range(T):
                    pe.wait_ge(v_set, b * T + t + 1)
                    terms = [(l, r) for k in range(KT) for l, r in halves(
                        x_hi[:, k, P * t:P * t + P], x_lo[:, k, P * t:P * t + P],
                        hi(k // 4)[:, 256 * (k % 4):256 * (k % 4) + 256], lo(k // 4)[:, 256 * (k % 4):256 * (k % 4) + 256])]
                    for k, (l, r) in enumerate(terms):
                        last = mm_(ps[:, 4 + t % 4, 0:256], l, r, start=k == 0, stop=k == len(terms) - 1)
                    last.then_inc(v_ps, 1)
                def projection(m, u, hf, uses=()):
                    r = (b * MT + m) * 2 + hf
                    pe.wait_ge(p_lo, r + 1)
                    terms = [(l, rr) for k in range(KT) for l, rr in halves(
                        hi(2 + u)[:, P * k:P * k + P], lo(2 + u)[:, P * k:P * k + P],
                        x_hi[:, k, H * hf:H * hf + H], x_lo[:, k, H * hf:H * hf + H])]
                    for k, (l, rr) in enumerate(terms):
                        last = mm_(ps[:, 2 * u + hf, :], l, rr, start=k == 0, stop=k == len(terms) - 1)
                        if k % 2 == 0 and k // 2 < len(uses):
                            maximum(0, 0, uses[k // 2], 0)
                    last.then_inc(p_ps, 1)

                def maximum(g, u, k, half):
                    gi = b * NKV + g
                    bank = ps[:, 6 + k % 2, :]
                    kind, n = USES[k]
                    if kind == "P":
                        qt, kh, j = PIECES[n]
                        w = piece_width(n)
                        if n == 0:
                            pe.wait_ge(qk_in[u][0], (b * (NKV // 2) + half + 1) * 96)
                        if n == FIRST:
                            pe.wait_ge(qk_in[u][1], (b * (NKV // 2) + half + 1) * 96)
                        pe.wait_ge(mx_rd, gi * NUSE + k + 1)
                        mm_(bank[:, 0:w], ring[0:96, 4 * u + j, P * qt:P * qt + P], kst[0:96, u, H * kh:H * kh + w],
                            start=True, stop=True).then_inc(mx_ps, 1)
                    else:
                        pe.wait_ge(m_neg, gi * 2 + n + 1)
                        pe.wait_ge(mx_rd, gi * NUSE + k + 1)
                        nc.tensor.transpose(bank[0:FIRST, 0:P], negm[:, u, n, :], ident[:]).then_inc(m_ps, 1)

                with pe.Fori(0, 3) as mm:
                    for u in range(2):
                        pe.wait_ge(w_lo, b * NCHUNK + C_M + mm * 2 + u + 1 + 2)
                        for hf in range(2):
                            projection(mm * 2 + u, u, hf)
                pe.wait_ge(y_lo, (b * 2 + 1) * T + 2)
                pe.wait_ge(v_set, (b + 1) * T + 4)
                for n in range(8):
                    m, u, hf = 6 + n // 2, n // 2 % 2, n % 2
                    if hf == 0:
                        pe.wait_ge(w_lo, b * NCHUNK + C_M + m + 1 + 2)
                    projection(m, u, hf, START[n])
                pe.wait_ge(p_cos, (b + 1) * (2 * MT))
                gate(k_ones, b + 1)

                def scores(g, u, n, own):
                    gi = b * NKV + g
                    kt = STEPS[n][1]
                    q0, w = step_range(n)
                    if n in (0, 4):
                        pe.wait_ge(m_in[n // 4], (gi + 1) * 32)
                    if n == 4:
                        pe.wait_ge(qk_in[u][1], (b * (NKV // 2) + own + 1) * 96)
                    pe.wait_ge(e_set, gi * NSTEP + n + 1)
                    for j in range(GQ):
                        last = mm_(ps[:, j, 0:w], kst[0:98, u, P * kt:P * kt + P], ring[0:98, 4 * u + j, q0:q0 + w], start=True, stop=True)
                    last.then_inc(st_ps, 1)

                def weighted(g, u, n, sums):
                    gi = b * NKV + g
                    qh, kt = STEPS[n]
                    q0, w = step_range(n)
                    c0 = q0 - H * qh
                    if not sums:
                        if n == 0:
                            pe.wait_ge(vg_set, gi + 1)
                        if kt == 0:
                            pe.wait_ge(o_nm, gi * 2 + qh + 1)
                        pe.wait_ge(e_set, gi * NSTEP + n + 2)
                        if n in DIAG:
                            pe.wait_ge(e_mask, gi * len(DIAG) + DIAG.index(n) + 1)
                    bank, lhs = (5, ones[:]) if sums else (4, vg[:, u, kt, :])
                    for j in range(GQ):
                        last = mm_(ps[HD * j:HD * j + HD, bank, c0:c0 + w], lhs, work[:, n % 3, j, 0:w],
                                   start=kt == 0, stop=kt == 4 * qh + 3, skip_group_check=True)
                    if sums and kt == 4 * qh + 3:
                        last.then_inc(o_ps, 1)

                def group(g, u, own, half, first=False, last=False):
                    for n in range(NSTEP):
                        todo = shares([] if last else uses_of(n), 4)

                        def maxima(k):
                            for x in todo[k]:
                                maximum(g + 1, 1 - u, x, half)

                        maxima(0)
                        scores(g, u, n, own)
                        before = (g, u, n - LAG) if n >= LAG else (g - 1, 1 - u, NSTEP + n - LAG)
                        maxima(1)
                        if n >= LAG or not first:
                            weighted(*before, False)
                            maxima(2)
                            weighted(*before, True)
                        else:
                            maxima(2)
                        maxima(3)

                group(0, 0, 0, 0, first=True)
                with pe.Fori(0, 3) as gg:
                    group(gg * 2 + 1, 1, gg, gg + 1)
                    group(gg * 2 + 2, 0, gg + 1, gg + 1)
                group(7, 1, 3, 4, last=True)
                for n in range(NSTEP - LAG, NSTEP):
                    weighted(7, 1, n, False)
                    weighted(7, 1, n, True)

                gate(o_lo, (b + 1) * (2 * NKV) + 2)
                with pe.Fori(0, 2) as nn:
                    for nu in range(2):
                        n = nn * 2 + nu
                        pe.wait_ge(w_lo, b * NCHUNK + C_O + n * 2 + 2 + 2)
                        for t in range(T):
                            pe.wait_ge(op_set, (b * 4 + n) * T + t + 1)
                            terms = [(l, r) for k in range(KT) for l, r in halves(
                                x_hi[:, k, P * t:P * t + P], x_lo[:, k, P * t:P * t + P],
                                hi(2 * nu + k // 4)[:, 256 * (k % 4):256 * (k % 4) + 256],
                                lo(2 * nu + k // 4)[:, 256 * (k % 4):256 * (k % 4) + 256])]
                            for k, (l, r) in enumerate(terms):
                                last = mm_(ps[:, t, 0:256], l, r, start=k == 0, stop=k == len(terms) - 1)
                            last.then_inc(op_ps, 1)
                gate(op_set, (b + 1) * 32 + 8)
                layernorm(b * 2 + 1)
                pe.wait_ge(y_lo, (b * 2 + 2) * T + 2)
                pe.wait_ge(down_in, (b + 1) * 16)
                pe.wait_ge(w_lo, b * NCHUNK + NCHUNK + 2)
                for pp in range(FH // 2):
                    for e in range(2):
                        hh = 2 * pp + e
                        pe.wait_ge(t_in[e], (b * (FH // 2) + pp + 1) * 16)
                        for hf in range(2):
                            pe.wait_ge(gel_set, b * (2 * FH) + 2 * hh + hf + 1)
                            for m in range(2):
                                w0 = FM * (hh % 4) + P * m
                                for k, w in enumerate((hi(hh // 4), lo(hh // 4))):
                                    last = mm_(ps[:, 2 * hf + m, :], w[:, w0:w0 + P], kst[:, e, H * hf:H * hf + H], start=k == 0, stop=k == 1)
                            last.then_inc(up_ps, 1)
                    pe.wait_ge(dn_set, b * (FH // 2) + pp + 1)
                    pe.wait_ge(gel_set, b * (2 * FH) + 4 * pp + 4 + 2)
                    for hf in range(2):
                        for m in range(2):
                            for e in range(2):
                                w0 = ((2 * pp + e) * 2 + m) * FD
                                last = mm_(ps[FD * e:FD * e + FD, 4 + 2 * (pp % 2) + hf, :], down_sb[:, w0:w0 + FD],
                                           gel[:, 2 * e + hf, m, :], start=m == 0, stop=m == 1, skip_group_check=True)
                    last.then_inc(dn_ps, 1)
                for t in range(T):
                    if t % 2 == 0:
                        pe.wait_ge(z_in[t // 2], (b + 1) * 16)
                    pe.wait_ge(f_set, b * T + t + 1)
                    for k in range(KT):
                        last = nc.tensor.transpose(ps[:, 2 * (t % 2) + k // 4, P * (k % 4):P * (k % 4) + P], z_sb[:, k, P * t:P * t + P], ident[:])
                    last.then_inc(f_ps, 1)


def _tiles(w, rows):
    k, n = w.shape[0] // P, w.shape[1] // rows
    return w.reshape(k, P, n, rows).transpose(2, 1, 0, 3).reshape(n, P, k * rows)


def kernel(**inputs):
    import numpy as np
    import concourse.bacc as bacc
    from concourse.bass_utils import run_bass_kernel_spmd as run

    a = {k: np.asarray(v) for k, v in inputs.items()}

    def columns(x):
        return np.ascontiguousarray(x.reshape(B * T, P).T)

    pairs = np.arange(HD).reshape(2, HD // 2).T.reshape(-1)

    def paired(w):
        return w.reshape(-1, HD, D)[:, pairs, :].reshape(-1, D)

    lora_b = np.stack([a["L0_tok_lora_B_cl"], a["L0_tok_lora_B_lm"], a["L0_tok_lora_B_cl_prime"]], 1)
    b_chunks = np.zeros((4, P, 1024), np.float32)
    b_chunks[:, :, 0:768] = lora_b.reshape(R, 3, 4, 256).transpose(2, 0, 1, 3).reshape(4, R, 768)
    wv = a["L0_attn_Wv"].T.reshape(2, 4, P, 256).transpose(0, 2, 1, 3).reshape(2, P, 1024)
    wk = _tiles(paired(a["L0_attn_Wk"]).T, P)
    wq = _tiles(paired(a["L0_attn_Wq"]).T, P)
    wo = a["L0_attn_Wo"].T.reshape(2, 4, P, 4, 256).transpose(3, 0, 2, 1, 4).reshape(8, P, 1024)
    up = a["L0_ffn_up"].reshape(4, 4, FD, FM).transpose(0, 2, 1, 3).reshape(4, FD, 4 * FM)
    up = np.concatenate([up, up], 1)
    chunks = np.concatenate([b_chunks, wv, wk, wq, wo, up], 0)
    down = a["L0_ffn_down"].reshape(FH, 2, P, FD).transpose(2, 0, 1, 3).reshape(P, FH * 2 * FD)

    inv = (np.float32(1.0) / np.float32(10000.0) ** (np.arange(0, HD, 2, dtype=np.float32) / np.float32(HD))).astype(np.float32)
    ang = np.outer(np.arange(S, dtype=np.float32), inv).astype(np.float32)
    cos = np.tile(np.repeat(np.cos(ang).T, 2, 0), (4, 1)).astype(np.float32)
    sin = (np.tile(np.repeat(np.sin(ang).T, 2, 0), (4, 1)) * np.tile(np.array([[1.0], [-1.0]]), (64, 1))).astype(np.float32)

    perm = a["L0_ffn_perm"].astype(np.int32) if a["L0_ffn_perm"].dtype != np.int32 else a["L0_ffn_perm"]
    perm_up = np.tile(perm.reshape(FH, FD), (1, 2)).T
    perm_down = perm.reshape(FH // 2, P).T
    arrays = {
        "ids": columns(a["x"]), "mask1": columns(a["mask_BS_i1_0"]), "mask0": columns(a["mask_BS_i0_1"]),
        "table_w": a["L0_tok_weight"], "table_a1": a["L0_tok_lora_A_cl"],
        "table_a23": np.concatenate([a["L0_tok_lora_A_lm"], a["L0_tok_lora_A_cl_prime"]], 1),
        "chunks": chunks, "down": down, "cos": cos, "sin": sin, "perm_up": perm_up, "perm_down": perm_down,
    }
    nc = bacc.Bacc("TRN2", target_bir_lowering=False, num_devices=1)
    feeds, aps = {}, []
    for name, arr in arrays.items():
        arr = np.ascontiguousarray(arr)
        feeds[f"{name}_dram"] = arr
        aps.append(nc.dram_tensor(f"{name}_dram", arr.shape, mybir.dt.from_np(arr.dtype), kind="ExternalInput").ap())
    out = nc.dram_tensor("out_dram", (B * S, D), F32, kind="ExternalOutput").ap()
    program(nc, *aps, out)
    r = run(nc, [feeds], core_ids=[0])
    return r.results[0]["out_dram"].reshape(B, S, D)
```

```python
import concourse.bass as bass
from concourse import mybir
from contextlib import ExitStack

F32 = mybir.dt.float32
F32R = mybir.dt.float32r
I32 = mybir.dt.int32
ALU = mybir.AluOpType
ACT = mybir.ActivationFunctionType
AX_X = mybir.AxisListType.X

P = 128
B, S, D = 4, 1024, 1024
V, R = 8000, 128
NH, NKV = 32, 8
HD = D // NH
GQ = NH // NKV
T = S // P
KT = D // P
H = S // 2
FH, FD, FM = 16, 64, 256
MT = 2 + NKV
SCALE = float(HD) ** -0.5
EPS = 1e-5
NEG = -2.0 ** 126

C_B, C_V, C_M, C_O, C_U, NCHUNK = 0, 4, 6, 16, 24, 28
STEPS = [(qh, kt) for qh in range(2) for kt in range(4 * (qh + 1))]
NSTEP = len(STEPS)
DIAG = [n for n, (qh, kt) in enumerate(STEPS) if kt >= 4 * qh]
PIECES = []
for _qt in range(T):
    for _kh in range(_qt // 4 + 1):
        _w = min(P * (_qt + 1) - H * _kh, H)
        _heads = {P: 4, 2 * P: 2}.get(_w, 1)
        PIECES += [("P", _qt, _kh, _w, _j, _heads) for _j in range(0, GQ, _heads)]
    if _qt == 3:
        FIRST = len(PIECES)
NPIECE = len(PIECES)
USES = PIECES[:FIRST + 3] + [("T", 0)] + PIECES[FIRST + 3:] + [("T", 1)]
NUSE = len(USES)
MROWS = 4 * GQ


def before(k):
    return sum(u[0] == "P" for u in USES[:k])


WEIGHTED = [[-2, -1], [], [0], [1], [2, 3], [], [4], [5], [6], [7], [8], [9]]


IDLE = 1500


def plan(first):
    width = [step_range(n)[1] for n in range(NSTEP)]
    begin = 3 if first else 0
    work = [[2 * width[n]] * 2 + [4 * width[m] for m in WEIGHTED[n] for _ in range(2)] +
            [0 if WEIGHTED[n] else IDLE] for n in range(NSTEP)]
    cost = [110 + (u[3] * u[5] if u[0] == "P" else 500) for u in USES]
    total, k, done, spent = sum(sum(x) for x in work[begin:]), 0, 0, 0
    result = []
    for n in range(NSTEP):
        row = []
        for x in work[n]:
            here = []
            while n >= begin and k < NUSE and done * total <= spent * sum(cost):
                here.append(k)
                done += cost[k]
                k += 1
            row.append(here)
            if n >= begin:
                spent += x
        result.append(row)
    result[-1][-1] += range(k, NUSE)
    return result


LAST = [(2, t) for t in range(3)] + [(x, t + 3 * (3 - x)) for t in range(T - 3) for x in (3, 2)] + [(3, t) for t in range(T - 3, T)]
F_PAIRS = [0, 6]
V_BANKS = [0, 1, 4, 5]
V_TURNS = {0: T - 2, 3: T - 1}


def step_range(n):
    qh, kt = STEPS[n]
    q0 = max(H * qh, P * kt)
    return q0, H * (qh + 1) - q0


PLAN = {first: plan(first) for first in (False, True)}
START = [[], []] + [list(range(NUSE * n // 10, NUSE * (n + 1) // 10)) for n in range(10)]


def program(nc, ids, mask1, mask0, table_w, table_a1, table_a23, chunks, down, cos, sin, perm_up, perm_down, out):
    with ExitStack() as ctx:
        def sb(name, shape, dt=F32):
            return ctx.enter_context(nc.sbuf_tensor(name, shape, dt))

        def sem(name):
            return ctx.enter_context(nc.semaphore(name))

        qk_dram = nc.dram_tensor("qk_dram", (2, MT * P, S), F32, kind="Internal").ap()
        y_dram = nc.dram_tensor("y_dram", (2 * D, S), F32, kind="Internal").ap()
        z_dram = nc.dram_tensor("z_dram", (D, S), F32, kind="Internal").ap()
        m_dram = nc.dram_tensor("m_dram", (2, 2, 2, MROWS, P), F32, kind="Internal").ap()

        h = sb("h", [P, T, D])
        x_hi = sb("x_hi", [P, KT, S], F32R)
        x_lo = sb("x_lo", [P, KT, S], F32R)
        ring = sb("ring", [P, 8, 1024], F32R)
        kst = sb("kst", [P, 2, S], F32R)
        work = sb("work", [P, 3, GQ, H])
        v_all = sb("v_all", [P, T, NKV * HD])
        vg = sb("vg", [P, 2, T, HD])
        raw = sb("raw", [P, 2, 1024])
        cos_sb = sb("cos_sb", [P, S])
        sin_sb = sb("sin_sb", [P, S])
        attn = sb("attn", [P, 2, H])
        r_hi = sb("r_hi", [P, 2, H], F32R)
        rden = sb("rden", [P, H // HD, HD])
        a_own = sb("a_own", [P, 2, 3 * R], F32R)
        rcol = sb("rcol", [P, H // HD, 1])
        ident = sb("ident", [P, P])
        ident_r = sb("ident_r", [P, P], F32R)
        causal = sb("causal", [P, P], F32R)
        ones = sb("ones", [P, HD])
        stats = sb("stats", [P, T, 2, 6])
        mv = sb("mv", [P, T, 2])
        ve = sb("ve", [P, T])
        sd = sb("sd", [P, T])
        rstd = sb("rstd", [P, T])
        nwt = sb("nwt", [P, T])
        mx = sb("mx", [P, 2, GQ, T, 2])
        negm = sb("negm", [P, 2, 2, MROWS])
        m_hi = sb("m_hi", [MROWS, 2, P], F32R)
        m_lo = sb("m_lo", [MROWS, 2, P], F32R)
        idx_raw = sb("idx_raw", [P, 3, B * T], I32)
        idx_neg = sb("idx_neg", [P, 3, B * T], I32)
        idx_all = sb("idx_all", [P, 3, (B + 1) * T], I32)
        idx_now = sb("idx_now", [P, 3, T], I32)
        pu = sb("pu", [P, FH], I32)
        pd = sb("pd", [P, FH // 2], I32)
        ps = ctx.enter_context(nc.psum_tensor("ps", [P, 8, 512], F32))

        r_lo = attn[:].bitcast(F32R)
        attn_flat = attn[:].rearrange("p u n -> p (u n)")
        a_rows = [attn_flat[:, 0:3 * R], attn_flat[:, 3 * R:6 * R], rden[:].rearrange("p c i -> p (c i)")[:, 0:3 * R],
                  vg[:].rearrange("p u t n -> p (u t n)")[:, 0:3 * R]]
        a_t = [a_own[:], r_hi[:].rearrange("p u n -> p (u n)")[:, 0:6 * R].rearrange("p (x n) -> p x n", x=2)]
        flat = work[:].rearrange("p a j n -> p (a j n)")
        y = flat[:, 2048:4096].rearrange("p (u n) -> p u n", u=2)
        r_cos = flat[:, 4096:5120].rearrange("p (u n) -> p u n", u=2)
        r_sin = flat[:, 5120:6144].rearrange("p (u n) -> p u n", u=2)
        r_swap = rden[:].rearrange("p c i -> p (c i)")
        gel = flat[:, 0:4096].rearrange("p (a m n) -> p a m n", a=4, m=2)
        d_out = flat[:, 4096:6144].rearrange("p (u n) -> p u n", u=2)
        b_w = ring[:, 0:6, :].rearrange("p a n -> p (a n)").rearrange("p (c x n) -> p c x n", c=4, x=2)
        down_sb = v_all[:].rearrange("p t n -> p (t n)")
        z_sb = x_hi[:].bitcast(F32)

        def hi(s):
            return ring[:, 2 * s, :]

        def lo(s):
            return ring[:, 2 * s + 1, :]

        def slot(c):
            if c < C_V:
                return b_w[:, c, 0, :], b_w[:, c, 1, :], 768
            if c == C_V + 1:
                return kst[:, 0, :], kst[:, 1, :], 1024
            s = {C_V: 3, C_M: 2, C_M + 1: 3}[c]
            return hi(s), lo(s), 1024

        def f32(ap):
            return ap.bitcast(F32)

        loaded = sem("loaded")
        tables_in = sem("tables_in")
        pu_set = sem("pu_set")
        consts = sem("consts")
        idx_ok = sem("idx_ok")
        prep = sem("prep")
        raw_in = [sem(f"raw_in{u}") for u in range(2)]
        w_hi = sem("w_hi")
        w_lo = sem("w_lo")
        idx_cp = sem("idx_cp")
        w_in = [sem(f"w_in{u}") for u in range(4)]
        a_in = [sem(f"a_in{u}") for u in range(4)]
        at_ps = sem("at_ps")
        at_hi = sem("at_hi")
        at_lo = sem("at_lo")
        emb_ps = sem("emb_ps")
        h_set = sem("h_set")
        st_set = sem("st_set")
        mv_set = sem("mv_set")
        ln_ve = sem("ln_ve")
        ln_sd = sem("ln_sd")
        ln_nw = sem("ln_nw")
        y_set = sem("y_set")
        y_ps = sem("y_ps")
        y_hi = sem("y_hi")
        y_lo = sem("y_lo")
        v_ps = sem("v_ps")
        v_set = sem("v_set")
        p_ps = sem("p_ps")
        p_cos = sem("p_cos")
        p_sin = sem("p_sin")
        p_swap = sem("p_swap")
        p_add = sem("p_add")
        p_hi = sem("p_hi")
        p_lo = sem("p_lo")
        p_out = [sem(f"p_out{u}") for u in range(2)]
        k_ones = sem("k_ones")
        qk_in = [[sem(f"qk_in{u}{x}") for x in range(2)] for u in range(2)]
        mx_ps = sem("mx_ps")
        mx_rd = sem("mx_rd")
        m_neg = sem("m_neg")
        m_ps = sem("m_ps")
        m_h = sem("m_h")
        m_st = sem("m_st")
        m_in = [sem(f"m_in{x}") for x in range(2)]
        st_ps = sem("st_ps")
        e_set = sem("e_set")
        e_mask = sem("e_mask")
        vg_set = sem("vg_set")
        o_ps = sem("o_ps")
        o_rd = sem("o_rd")
        o_nm = sem("o_nm")
        o_hi = sem("o_hi")
        o_lo = sem("o_lo")
        op_ps = sem("op_ps")
        op_set = sem("op_set")
        y_out = sem("y_out")
        down_in = sem("down_in")
        t_in = [sem(f"t_in{u}") for u in range(4)]
        up_ps = sem("up_ps")
        gel_set = sem("gel_set")
        dn_ps = sem("dn_ps")
        dn_set = sem("dn_set")
        z_out = [sem(f"z_out{u}") for u in range(2)]
        z_in = [sem(f"z_in{x}") for x in range(4)]
        f_ps = sem("f_ps")
        f_set = sem("f_set")
        stored = [sem(f"stored{x}") for x in range(4)]
        gate_pool = sem("gate_pool")
        gate_act = sem("gate_act")
        gate_dve = sem("gate_dve")
        gate_pe = sem("gate_pe")
        gate_sp = sem("gate_sp")

        block = ctx.enter_context(nc.Block())

        @block.sync
        def _(sp):
            def gate(s, value):
                sp.wait_ge(s, value)
                sp.sem_inc(gate_sp, 1)

            for x in range(4):
                sp.sem_inc(stored[x], 32)
            for dst, src in ((idx_raw[:, 0, :], ids), (idx_raw[:, 1, :], mask1), (idx_raw[:, 2, :], mask0)):
                sp.dma_start(dst, src).then_inc(loaded, 16)

            def load_chunk(b, c, u):
                gate(w_lo, b * NCHUNK + c + 1)
                sp.dma_start(raw[:, u, :], chunks[bass.ds(c, 1), :, :].rearrange("o p n -> (o p) n")).then_inc(raw_in[u], 16)

            def load_group(b, g, u, x):
                cols = slice(H * x, H * x + H)
                for row, half in ((0, 0), (1, 1), (2, 0)):
                    sp.dma_start(f32(ring[HD * row:HD * row + HD, 4 * u:4 * u + GQ, cols]),
                                 qk_dram[half, bass.ds((2 + g) * P, P), cols].rearrange("(j d) n -> d j n", d=HD)).then_inc(qk_in[u][x], 16)
                for row, half in ((0, 0), (1, 0), (2, 1)):
                    sp.dma_start(f32(kst[HD * row:HD * row + HD, u, cols]),
                                 qk_dram[half, bass.ds(g * HD, HD), cols]).then_inc(qk_in[u][x], 16)

            def max_rows(gi, u, x):
                gate(mx_rd, gi * NUSE + USES.index(("T", x)) + 3)
                sp.dma_start(m_dram[0, u, x, :, :], f32(m_hi[:, x, :])).then_inc(m_st, 16)
                sp.dma_start(m_dram[1, u, x, :, :], f32(m_lo[:, x, :])).then_inc(m_st, 16)
                gate(m_st, (gi * 2 + x + 1) * 32)
                for half in range(2):
                    sp.dma_start(f32(ring[96 + half:97 + half, 4 * u:4 * u + GQ, H * x:H * x + H]),
                                 m_dram[half, u, x, :, :].rearrange("(o j t) n -> o j (t n)", o=1, j=GQ)).then_inc(m_in[x], 16)

            for c in range(C_M):
                load_chunk(0, c, c % 2)
                if c == 1:
                    for dst, src in ((cos_sb[:], cos), (sin_sb[:], sin), (pu[:], perm_up), (pd[:], perm_down)):
                        sp.dma_start(dst, src).then_inc(tables_in, 16)
            with sp.Fori(0, B) as b:
                for c in range(C_M, 10):
                    load_chunk(b, c, c % 2)
                def store(m):
                    for hf in range(2):
                        gate(p_lo, (b * MT + m) * 2 + hf + 3)
                        for x, src in ((0, r_hi), (1, r_lo)):
                            sp.dma_start(qk_dram[x, bass.ds(m * P, P), H * hf:H * hf + H], f32(src[:, hf, :])).then_inc(p_out[hf], 16)

                with sp.Fori(0, 2) as mm:
                    for u in range(2):
                        store(mm * 2 + u)
                        load_chunk(b, mm * 2 + u + 10, u)
                for hf in range(2):
                    gate(p_out[hf], (b * MT + 4) * 32 + 32)
                for x in range(2):
                    load_group(b, 0, 0, x)
                for m in range(4, MT - 1):
                    store(m)
                    if m < 8:
                        load_chunk(b, m + 10, m % 2)
                max_rows(b * NKV, 0, 0)
                gate(p_ps, (b + 1) * (2 * MT))
                for x in range(2):
                    load_group(b, 1, 1, x)
                store(MT - 1)
                for hf in range(2):
                    gate(p_out[hf], (b + 1) * (MT * 32) + 32)
                max_rows(b * NKV, 0, 1)

                def group(g, u, ahead=True):
                    gi = b * NKV + g
                    max_rows(gi + 1, 1 - u, 0)
                    if ahead:
                        gate(st_ps, gi * NSTEP + 8)
                        load_group(b, g + 2, u, 0)
                        gate(st_ps, gi * NSTEP + NSTEP)
                        load_group(b, g + 2, u, 1)
                    max_rows(gi + 1, 1 - u, 1)

                with sp.Fori(0, 3) as gg:
                    for u in range(2):
                        group(gg * 2 + u, u)
                group(6, 0, ahead=False)
                for c in range(18, 20):
                    load_chunk(b, c, c % 2)
                gate(o_ps, (b + 1) * (2 * NKV))
                sp.dma_start(down_sb, down).then_inc(down_in, 16)
                with sp.Fori(0, 3) as n:
                    for u in range(2):
                        load_chunk(b, n * 2 + u + 20, u)
                with sp.Fori(0, T) as t:
                    gate(y_lo, (b * 2 + 1) * T + t + 3)
                    for x, src in enumerate((x_hi, x_lo)):
                        sp.dma_start(y_dram[D * x:D * x + D, bass.ds(t * P, P)].rearrange("(k p) n -> p k n", p=P),
                                     f32(src[:, :, bass.ds(t * P, P)])).then_inc(y_out, 16)
                for c in range(C_U + 2, NCHUNK):
                    load_chunk(b, c, c % 2)
                for c in range(C_M):
                    load_chunk(b + 1, c, c % 2)
                gate(y_out, (b + 1) * (32 * T))
                for u in range(2):
                    gate(z_out[u], (b + 1) * (16 * FH // 4))
                for x in range(4):
                    cols = slice(2 * P * x, 2 * P * x + 2 * P)
                    sp.dma_start(z_sb[:, :, cols], z_dram[:, cols].rearrange("(k p) n -> p k n", p=P)).then_inc(z_in[x], 16)
                for t in range(T):
                    gate(f_set, b * T + t + 3)
                    sp.dma_start(out[bass.ds((b * T + t) * P, P), :], h[:, t, :]).then_inc(stored[t // 2], 16)
            for x in range(4):
                sp.wait_ge(stored[x], 32 * (B + 1))

        @block.gpsimd
        def _(pool):
            pool.sem_inc(w_lo, 2)
            pool.sem_inc(p_lo, 2)
            pool.sem_inc(o_lo, 2)
            pool.memset(ident[:], 0.0).then_inc(consts, 1)
            scratch = attn[:, 0, 0:P]
            pool.memset(scratch, 0.0).then_inc(consts, 1)
            pool.memset(ones[:], 1.0).then_inc(consts, 1)
            pool.wait_ge(consts, 3)
            pool.affine_select(out=ident[:], in_=ident[:], compare_op=ALU.not_equal, fill=1.0, base=0,
                               pattern=[[-1, P]], channel_multiplier=1).then_inc(consts, 1)
            pool.affine_select(out=scratch, in_=scratch, compare_op=ALU.is_ge, fill=NEG, base=0,
                               pattern=[[-1, P]], channel_multiplier=1).then_inc(consts, 1)
            pool.wait_ge(consts, 5)
            pool.tensor_copy(ident_r[:], ident[:]).then_inc(consts, 1)
            pool.tensor_copy(causal[:], scratch).then_inc(consts, 1)
            pool.wait_ge(consts, 7)
            pool.wait_ge(idx_ok, 1)

            def gate(s, value):
                pool.wait_ge(s, value)
                pool.sem_inc(gate_pool, 1)

            def split_lo(b, c, s, u):
                gate(w_hi, b * NCHUNK + c + 1)
                pool.tensor_tensor(lo(s), raw[:, u, :], f32(hi(s)), ALU.subtract).then_inc(w_lo, 1)

            def first_lo(b, c):
                dst_hi, dst_lo, n = slot(c)
                gate(w_hi, b * NCHUNK + c + 1)
                pool.tensor_tensor(dst_lo, raw[:, c % 2, 0:n], f32(dst_hi), ALU.subtract).then_inc(w_lo, 1)

            def lora_rows(t):
                u = t % 4
                for dst, table, k in ((a_rows[u][:, 0:R], table_a1, 1), (a_rows[u][:, R:3 * R], table_a23, 2)):
                    pool.indirect_dma_start(dst, None, table, bass.IndirectOffsetOnAxis(ap=idx_now[:, k, t:t + 1], axis=0)).then_inc(a_in[u], 16)

            pool.tensor_copy(idx_now[:], idx_all[:, :, 0:T]).then_inc(idx_cp, 1)
            pool.wait_ge(idx_cp, 1)
            for t in range(4):
                lora_rows(t)
            for c in range(C_M):
                first_lo(0, c)

            with pool.Fori(0, B) as b:
                for t in range(T):
                    if t >= 4:
                        gate(at_ps, b * T + t - 4 + 1)
                        lora_rows(t)
                        gate(h_set, b * T + t - 4 + 3)
                    if t % 2 == 0:
                        gate(stored[t // 2], (b + 1) * 32)
                    pool.indirect_dma_start(h[:, t, :], None, table_w, bass.IndirectOffsetOnAxis(ap=idx_now[:, 0, t:t + 1], axis=0)).then_inc(w_in[t % 4], 16)
                for c in (C_M, C_M + 1):
                    first_lo(b, c)

                gate(v_ps, (b + 1) * T)
                gate(w_lo, b * NCHUNK + 8 + 2)
                pool.memset(f32(kst[96:98, :, :]), 1.0).then_inc(k_ones, 1)
                gate(k_ones, b + 1)

                def rotated_lo(m, hf):
                    gate(p_hi, (b * MT + m) * 2 + hf + 1)
                    pool.tensor_tensor(r_lo[:, hf, :], r_cos[:, hf, :], f32(r_hi[:, hf, :]), ALU.subtract).then_inc(p_lo, 1)

                with pool.Fori(0, MT // 2 - 1) as mm:
                    for u in range(2):
                        rotated_lo(mm * 2 + u, 0)
                        split_lo(b, mm * 2 + u + 8, 2 + u, u)
                        rotated_lo(mm * 2 + u, 1)
                for u in range(2):
                    rotated_lo(MT - 2 + u, 0)
                    rotated_lo(MT - 2 + u, 1)

                def values(g, u):
                    pool.tensor_copy(vg[:, u, :, :], v_all[:, :, bass.ds(g * HD, HD)]).then_inc(vg_set, 1)

                def group(g, u, first=False, last=False):
                    gi = b * NKV + g
                    for n in range(NSTEP):
                        if n in DIAG:
                            gate(e_set, gi * NSTEP + n + 2)
                            pool.affine_select(out=work[:, n % 3, :, 0:P], in_=work[:, n % 3, :, 0:P], compare_op=ALU.is_ge,
                                               fill=0.0, base=0, pattern=[[0, GQ], [1, P]], channel_multiplier=-1).then_inc(e_mask, 1)
                        if n == 4 and not first:
                            split_attn(g - 1, 1)
                        if n == 5 and not last:
                            if not first:
                                gate(o_ps, gi * 2)
                            values(g + 1, 1 - u)
                        if n == 7:
                            split_attn(g, 0)
                        if last and n in (5, 6):
                            c = C_O + n - 5
                            split_lo(b, c, n - 5, c % 2)

                def split_attn(g, qh):
                    k = (b * NKV + g) * 2 + qh
                    gate(o_hi, k + 1)
                    col = x_lo[:, bass.ds(g, 1), H * qh:H * qh + H].rearrange("p o n -> p (o n)")
                    src = x_hi[:, bass.ds(g, 1), H * qh:H * qh + H].rearrange("p o n -> p (o n)")
                    pool.tensor_tensor(col, attn[:, qh, :], f32(src), ALU.subtract).then_inc(o_lo, 1)

                gate(v_set, (b + 1) * T + 4)
                values(0, 0)
                group(0, 0, first=True)
                with pool.Fori(0, 3) as gg:
                    group(gg * 2 + 1, 1)
                    group(gg * 2 + 2, 0)
                group(7, 1, last=True)
                split_attn(7, 1)

                for c in range(18, C_U):
                    split_lo(b, c, c % 4, c % 2)
                for c in range(C_U, C_U + 2):
                    split_lo(b, c, c % 4, c % 2)
                gate(y_out, (b + 1) * (32 * T))
                pool.wait_ge(pu_set, 1)
                pool.tensor_copy(idx_now[:], idx_all[:, :, bass.ds((b + 1) * T, T)]).then_inc(idx_cp, 1)
                gate(idx_cp, b + 2)

                def gather(hh):
                    pool.indirect_dma_start(f32(x_lo[:, hh % 4, :]), None, y_dram, bass.IndirectOffsetOnAxis(ap=pu[:, hh:hh + 1], axis=0)).then_inc(t_in[hh % 4], 16)

                for hh in range(4):
                    gather(hh)
                for c in range(C_U + 2, NCHUNK):
                    split_lo(b, c, c % 4, c % 2)
                for pp in range(FH // 2):
                    for hh in (2 * pp, 2 * pp + 1):
                        if hh + 4 < FH:
                            gate(up_ps, (b * (FH // 2) + pp) * 4 + 3 + hh % 2)
                            gather(hh + 4)
                    if 2 <= pp < 6:
                        lora_rows(pp - 2)
                    for c in {3: (0,), 5: (1,), 6: (2,), 7: (3,)}.get(pp, ()):
                        first_lo(b + 1, c)
                    gate(dn_set, (b * (FH // 2) + pp + 1) * 2 + 4)
                    pool.indirect_dma_start(z_dram, bass.IndirectOffsetOnAxis(ap=pd[:, pp:pp + 1], axis=0),
                                            d_out[:, pp % 2, :], None).then_inc(z_out[pp % 2], 16)
                for c in range(C_V, C_M):
                    first_lo(b + 1, c)
            for u in range(4):
                pool.wait_ge(a_in[u], (2 * B + 1) * 32)

        @block.scalar
        def _(act):
            act.sem_inc(v_set, 4)
            act.sem_inc(e_set, 1)
            act.sem_inc(gel_set, 2)

            def gate(s, value):
                act.wait_ge(s, value)
                act.sem_inc(gate_act, 1)

            def split_hi(b, pair, s, u):
                gate(raw_in[u], (b * (NCHUNK // 2) + pair + 1) * 16)
                act.activation(hi(s), raw[:, u, :], ACT.Copy).then_inc(w_hi, 1)

            def first_hi(b, c):
                dst_hi, _, n = slot(c)
                gate(raw_in[c % 2], (b * (NCHUNK // 2) + c // 2 + 1) * 16)
                act.activation(dst_hi, raw[:, c % 2, 0:n], ACT.Copy).then_inc(w_hi, 1)

            def root(ln, t):
                gate(ln_ve, ln * T + t + 1)
                act.activation(sd[:, t:t + 1], ve[:, t:t + 1], ACT.Sqrt).then_inc(ln_sd, 1)

            def stream_hi(ln, t, pair):
                gate(y_ps, ln * T + t + 1)
                act.activation(x_hi[:, :, P * t:P * t + P], ps[:, pair:pair + 2, :].rearrange("p a (k n) -> p (a k) n", n=P), ACT.Copy).then_inc(y_hi, 1)

            def lora_hi(b, t):
                gate(at_ps, b * T + t + 1)
                act.activation(a_t[t % 2][:, 0, :], ps[:, t % 2, 0:3 * R], ACT.Copy).then_inc(at_hi, 1)

            for c in range(C_V):
                first_hi(0, c)
            for t in range(2):
                lora_hi(0, t)
            for c in range(C_V, C_M):
                first_hi(0, c)

            with act.Fori(0, B) as b:
                ln = b * 2
                for t in range(1, T):
                    if 1 < t + 1 < T:
                        lora_hi(b, t + 1)
                    root(ln, t - 1)
                    if t >= 2:
                        stream_hi(ln, t - 2, 6)
                root(ln, T - 1)
                act.wait_ge(emb_ps, (b + 1) * T)
                first_hi(b, C_M)
                for t in range(T):
                    act.wait_ge(v_ps, b * T + t + 1)
                    act.activation(v_all[:, t, :], ps[:, V_BANKS[t % 4], 0:NKV * HD], ACT.Copy).then_inc(v_set, 1)
                    if t in V_TURNS:
                        stream_hi(ln, V_TURNS[t], 6)
                first_hi(b, C_M + 1)

                def rotated_hi(m, hf):
                    gate(p_add, (b * MT + m) * 2 + hf + 1)
                    act.wait_ge(p_out[hf], (b * MT + m + 1) * 32)
                    act.activation(r_hi[:, hf, :], r_cos[:, hf, :], ACT.Copy).then_inc(p_hi, 1)

                with act.Fori(0, MT // 2 - 1) as mm:
                    for u in range(2):
                        rotated_hi(mm * 2 + u, 0)
                        gate(p_ps, (b * MT + mm * 2 + u + 1) * 2)
                        split_hi(b, mm + 4, 2 + u, u)
                        rotated_hi(mm * 2 + u, 1)
                for u in range(2):
                    rotated_hi(MT - 2 + u, 0)
                    rotated_hi(MT - 2 + u, 1)

                def group(g, first=False, last=False):
                    gi = b * NKV + g
                    for n in range(NSTEP):
                        w = step_range(n)[1]
                        if first and n == 2:
                            gate(p_lo, (b + 1) * (2 * MT) + 2)
                        act.wait_ge(st_ps, gi * NSTEP + n + 1)
                        act.activation(work[:, n % 3, :, 0:w], ps[:, 0:GQ, 0:w], ACT.Exp, scale=SCALE).then_inc(e_set, 1)
                        if n == 2 and not first:
                            attn_hi(g - 1, 1)
                        if n == 6:
                            attn_hi(g, 0)
                        if last and n in (4, 5):
                            split_hi(b, C_O // 2, n - 4, n - 4)

                def attn_hi(g, qh):
                    gate(o_nm, (b * NKV + g) * 2 + qh + 2)
                    act.activation(x_hi[:, bass.ds(g, 1), H * qh:H * qh + H].rearrange("p o n -> p (o n)"),
                                   attn[:, qh, :], ACT.Copy).then_inc(o_hi, 1)

                group(0, first=True)
                with act.Fori(0, 3) as gg:
                    group(gg * 2 + 1)
                    group(gg * 2 + 2)
                group(7, last=True)
                attn_hi(7, 1)
                gate(st_ps, (b + 1) * (NKV * NSTEP))
                for c in range(18, 20):
                    split_hi(b, c // 2, c - 16, c % 2)
                def next_hi(c):
                    split_hi(b, c // 2, c % 4, c % 2)

                for c in range(20, 24):
                    gate(op_ps, (b * 4 + (c - 20) // 2 + 1) * T)
                    next_hi(c)
                ln = b * 2 + 1
                for t in range(T + 2):
                    if t >= 2:
                        stream_hi(ln, t - 2, 4 + 2 * (t % 2))
                    if t < T:
                        root(ln, t)
                    else:
                        next_hi(C_U + t - T)
                for c in range(C_U + 2, NCHUNK):
                    next_hi(c)
                for pp in range(FH // 2):
                    for c, done in {3: ((0, 2),), 5: ((1, 4),), 6: ((2, 6),), 7: ((3, 6),)}.get(pp, ()):
                        gate(up_ps, (b * (FH // 2) + done) * 4)
                        first_hi(b + 1, c)
                    for hf in range(2):
                        for e in range(2):
                            n = (b * (FH // 2) + pp) * 4 + 2 * hf + e
                            act.wait_ge(up_ps, n + 1)
                            if pp and e == 0:
                                act.wait_ge(dn_ps, (b * (FH // 2) + pp - 1) * 2 + hf + 1)
                            act.activation(gel[:, 2 * hf + e, :, :], ps[:, 2 * e:2 * e + 2, :], ACT.Gelu).then_inc(gel_set, 1)
                for t in range(2):
                    lora_hi(b + 1, t)
                gate(up_ps, (b + 1) * (2 * FH))
                first_hi(b + 1, C_V)
                first_hi(b + 1, C_V + 1)

        @block.vector
        def _(dve):
            v = nc.vector
            dve.sem_inc(h_set, 2)
            dve.sem_inc(y_lo, 2)
            dve.sem_inc(p_out[0], 32)
            dve.sem_inc(p_out[1], 32)
            dve.sem_inc(mx_rd, 2)
            dve.sem_inc(o_nm, 1)
            dve.sem_inc(op_set, 8)
            dve.sem_inc(dn_set, 4)
            dve.sem_inc(f_set, 2)

            def gate(s, value):
                dve.wait_ge(s, value)
                dve.sem_inc(gate_dve, 1)

            chain = [0]

            def link(ins):
                chain[0] += 1
                ins.then_inc(prep, 1)
                dve.wait_ge(prep, chain[0])

            dve.wait_ge(loaded, 3 * 16)
            link(v.memset(mx[:], NEG))
            link(v.tensor_tensor(idx_raw[:, 1, :], idx_raw[:, 1, :], idx_raw[:, 0, :], ALU.mult))
            link(v.tensor_tensor(idx_raw[:, 2, :], idx_raw[:, 2, :], idx_raw[:, 0, :], ALU.mult))
            link(v.tensor_scalar(idx_neg[:], idx_raw[:], 0, V, ALU.is_lt, ALU.mult))
            link(v.tensor_tensor(idx_raw[:], idx_raw[:], idx_neg[:], ALU.add))
            link(v.memset(idx_all[:, :, B * T:(B + 1) * T], 0))
            v.tensor_scalar(idx_all[:, :, 0:B * T], idx_raw[:], 0, V - 1, ALU.max, ALU.min).then_inc(idx_ok, 1)
            dve.wait_ge(tables_in, 4 * 16)
            v.tensor_scalar(pu[FD:P, :], pu[FD:P, :], D, None, ALU.add).then_inc(pu_set, 1)

            def tile_stats(ln, t, k):
                v.bn_stats(out=stats[:, t, k, :], in_=h[:, t, H * k:H * k + H]).then_inc(st_set, 1)

            def tile_mean(ln, t):
                gate(st_set, (ln * T + t) * 2 + 2)
                v.bn_aggr(out=mv[:, t, :], in_=stats[:, t, :, :].rearrange("p k s -> p (k s)")).then_inc(mv_set, 1)

            def tile_var(ln, t):
                gate(mv_set, ln * T + t + 1)
                v.tensor_scalar(ve[:, t:t + 1], mv[:, t, 1:2], EPS, None, ALU.add).then_inc(ln_ve, 1)

            def newton(ln, t, step):
                n = ln * T + t
                one, inv, nw = ve[:, t:t + 1], rstd[:, t:t + 1], nwt[:, t:t + 1]
                if step == 0:
                    gate(ln_sd, n + 1)
                    v.reciprocal(inv, sd[:, t:t + 1]).then_inc(ln_nw, 1)
                    return
                gate(ln_nw, n * 4 + step)
                if step == 1:
                    v.scalar_tensor_tensor(nw, inv, inv, one, ALU.mult, ALU.mult).then_inc(ln_nw, 1)
                if step == 2:
                    v.tensor_scalar(nw, nw, -0.5, 1.5, ALU.mult, ALU.add).then_inc(ln_nw, 1)
                if step == 3:
                    v.tensor_tensor(inv, inv, nw, ALU.mult).then_inc(ln_nw, 1)

            def normalise(ln, t):
                gate(ln_nw, (ln * T + t) * 4 + 4)
                v.tensor_scalar(y[:, t % 2, :], h[:, t, :], mv[:, t, 0:1], rstd[:, t:t + 1], ALU.subtract, ALU.mult).then_inc(y_set, 1)

            def layernorm_step(ln, t, extra=None):
                small = [lambda k=k: newton(ln, t - 1, k) for k in range(4)] if t >= 1 else [lambda: None] * 4
                big = []
                if t < T:
                    big = [lambda: tile_stats(ln, t, 0), lambda: tile_stats(ln, t, 1)]
                if extra:
                    big.append(extra)
                for k in range(4):
                    small[k]()
                    if big:
                        big.pop(0)()
                if t < T:
                    tile_mean(ln, t)
                if t >= 1:
                    normalise(ln, t - 1)
                if t < T:
                    tile_var(ln, t)

            def stream_lo(ln, t, pair):
                gate(y_hi, ln * T + t + 1)
                cols = slice(P * t, P * t + P)
                v.tensor_tensor(x_lo[:, :, cols], ps[:, pair:pair + 2, :].rearrange("p a (k n) -> p (a k) n", n=P),
                                f32(x_hi[:, :, cols]), ALU.subtract).then_inc(y_lo, 1)

            def lora_lo(b, t):
                gate(at_hi, b * T + t + 1)
                v.tensor_tensor(a_t[t % 2][:, 1, :], ps[:, t % 2, 0:3 * R], f32(a_t[t % 2][:, 0, :]), ALU.subtract).then_inc(at_lo, 1)

            for t in range(2):
                lora_lo(0, t)
            with dve.Fori(0, B) as b:
                lora_lo(b, 2)
                for t in range(T + 1):
                    n = b * T + t
                    if t >= 3:
                        stream_lo(b * 2, t - 3, 6)
                    if t < T:
                        gate(w_in[t % 4], (b * 2 + t // 4 + 1) * 16)
                        gate(emb_ps, n + 1)
                        two = 2 + 2 * (t % 2)
                        v.scalar_tensor_tensor(h[:, t, :], ps[:, two:two + 2, :].rearrange("p a n -> p (a n)"), 2.0, h[:, t, :],
                                               ALU.mult, ALU.add).then_inc(h_set, 1)
                        gate(h_set, n + 3)
                    layernorm_step(b * 2, t, (lambda: lora_lo(b, t + 2)) if 2 < t + 2 < T else None)
                for t in (T - 2, T - 1):
                    stream_lo(b * 2, t, 6)
                def rotate(m, u, hf, between=()):
                    fill = list(between)

                    def one():
                        if fill:
                            maximum(0, 0, fill.pop(0))

                    r = (b * MT + m) * 2 + hf
                    gate(p_lo, r + 1)
                    gate(p_ps, r + 1)
                    bank = ps[:, 2 * u + hf, :]
                    v.tensor_tensor(r_sin[:, hf, :], bank, sin_sb[:, H * hf:H * hf + H], ALU.mult).then_inc(p_sin, 1)
                    v.tensor_tensor(r_cos[:, hf, :], bank, cos_sb[:, H * hf:H * hf + H], ALU.mult).then_inc(p_cos, 1)
                    one()
                    gate(p_sin, r + 1)
                    v.stream_shuffle(r_swap, r_sin[:, hf, :], [i ^ 1 for i in range(32)]).then_inc(p_swap, 1)
                    one()
                    gate(p_cos, r + 1)
                    gate(p_swap, r + 1)
                    v.tensor_tensor(r_cos[:, hf, :], r_cos[:, hf, :], r_swap, ALU.add).then_inc(p_add, 1)
                    while fill:
                        one()

                def maximum(g, u, k):
                    gi = b * NKV + g
                    bank = ps[:, 6 + k % 2, :]
                    if USES[k][0] == "P":
                        _, qt, kh, w, j, heads = USES[k]
                        n = before(k)
                        gate(mx_ps, gi * NPIECE + n + 1)
                        v.tensor_reduce(out=mx[:, u, j:j + heads, qt, kh], in_=bank[:, 0:heads * w].rearrange("p (j n) -> p j n", j=heads),
                                        axis=AX_X, op=ALU.max).then_inc(mx_rd, 1)
                        if n in (FIRST - 1, NPIECE - 1):
                            x = int(n >= FIRST)
                            gate(mx_rd, gi * NUSE + k + 3)
                            v.tensor_reduce(out=negm[:, u, x, :].rearrange("p (j t) -> p j t", j=GQ), in_=mx[:, u, :, 4 * x:4 * x + 4, :],
                                            axis=AX_X, op=ALU.max, negate=True).then_inc(m_neg, 1)
                    else:
                        x = USES[k][1]
                        gate(m_ps, gi * 2 + x + 1)
                        v.tensor_copy(m_hi[:, x, :], bank[0:MROWS, 0:P]).then_inc(m_h, 1)
                        gate(m_h, gi * 2 + x + 1)
                        v.tensor_tensor(m_lo[:, x, :], bank[0:MROWS, 0:P], f32(m_hi[:, x, :]), ALU.subtract).then_inc(mx_rd, 1)

                def normalise_attn(g, qh, between=()):
                    fill = list(between)

                    def one():
                        if fill:
                            maximum(*fill.pop(0))

                    k = (b * NKV + g) * 2 + qh
                    gate(o_ps, k + 1)
                    gate(o_lo, k + 1)
                    v.transpose(rden[:].rearrange("p c i -> p (c i)"), ps[:, 5, :]).then_inc(o_rd, 1)
                    one()
                    gate(o_rd, k * 3 + 1)
                    v.reciprocal(rcol[:], rden[:, :, 0:1]).then_inc(o_rd, 1)
                    one()
                    gate(o_rd, k * 3 + 2)
                    v.transpose(rden[:], rcol[:].to_broadcast([P, H // HD, HD])).then_inc(o_rd, 1)
                    one()
                    gate(o_rd, k * 3 + 3)
                    v.tensor_tensor(attn[:, qh, :], ps[:, 4, :], rden[:].rearrange("p c i -> p (c i)"), ALU.mult).then_inc(o_nm, 1)
                    while fill:
                        one()

                with dve.Fori(0, 2) as mm:
                    for u in range(2):
                        for hf in range(2):
                            rotate(mm * 2 + u, u, hf)
                for n in range(12):
                    rotate(4 + n // 2, n // 2 % 2, n % 2, START[n + 1] if n < 11 else ())

                def group(g, u, first=False, last=False):
                    for n in range(NSTEP):
                        todo = [] if last else [(g + 1, 1 - u, k) for here in PLAN[first][n] for k in here]
                        if n == 1 and not first:
                            normalise_attn(g - 1, 1, todo)
                        elif n == 5:
                            normalise_attn(g, 0, todo)
                        else:
                            for use in todo:
                                maximum(*use)

                group(0, 0, first=True)
                with dve.Fori(0, 3) as gg:
                    group(gg * 2 + 1, 1)
                    group(gg * 2 + 2, 0)
                group(7, 1, last=True)
                normalise_attn(7, 1)

                def add_output(n, t, bank, count):
                    cols = h[:, t, bass.ds(n * 256, 256)]
                    gate(op_ps, b * 4 * T + count + 1)
                    v.tensor_tensor(cols, ps[:, bank, 0:256], cols, ALU.add).then_inc(op_set, 1)

                with dve.Fori(0, 2) as n:
                    for t in range(T):
                        add_output(n, t, t, n * T + t)
                for t in range(T + 1):
                    if t >= 3:
                        stream_lo(b * 2 + 1, t - 3, 4 + 2 * ((t - 3) % 2))
                    if t < T:
                        done = [LAST.index((3, x)) + 1 if x >= 0 else 0 for x in (t - 1, t)]
                        for i in range(*done):
                            add_output(*LAST[i], i % 4, 2 * T + i)
                        gate(op_set, (b * 4 + 2) * T + done[1] + 8)
                    layernorm_step(b * 2 + 1, t)
                for t in (T - 2, T - 1):
                    stream_lo(b * 2 + 1, t, 4 + 2 * (t % 2))
                for pp in range(FH // 2):
                    u = pp % 2
                    if pp >= 2:
                        gate(z_out[u], (b * (FH // 4) + pp // 2) * 16)
                    for hf in range(2):
                        gate(dn_ps, (b * (FH // 2) + pp) * 2 + hf + 1)
                        v.tensor_copy(d_out[:, u, H * hf:H * hf + H], ps[:, 4 + 2 * u + hf, :]).then_inc(dn_set, 1)
                        if pp == FH // 2 - 1:
                            lora_lo(b + 1, hf)
                with dve.Fori(0, T // 2) as tt:
                    for u in range(2):
                        row = h[:, bass.ds(tt * 2 + u, 1), :].rearrange("p o n -> p (o n)")
                        gate(f_ps, b * T + tt * 2 + u + 1)
                        v.tensor_tensor(row, ps[:, F_PAIRS[u]:F_PAIRS[u] + 2, :].rearrange("p a n -> p (a n)"), row, ALU.add).then_inc(f_set, 1)

        @block.tensor
        def _(pe):
            mm_ = nc.tensor.matmul

            def gate(s, value):
                pe.wait_ge(s, value)
                pe.sem_inc(gate_pe, 1)

            pe.wait_ge(consts, 7)

            def halves(lhs_hi, lhs_lo, rhs_hi, rhs_lo):
                return ((lhs_hi, rhs_hi), (lhs_lo, rhs_hi), (lhs_hi, rhs_lo))

            def turn_stream(ln, t, pair, ahead):
                n = ln * T + t
                pe.wait_ge(y_set, n + 1)
                pe.wait_ge(y_lo, n + 3 - ahead)
                for k in range(KT):
                    last = nc.tensor.transpose(ps[:, pair + k // 4, P * (k % 4):P * (k % 4) + P], y[:, t % 2, P * k:P * k + P], ident[:])
                last.then_inc(y_ps, 1)

            def turn_rows(b, t):
                pe.wait_ge(a_in[t % 4], (b * 2 + t // 4 + 1) * 32)
                for k in range(3):
                    last = nc.tensor.transpose(ps[:, t % 2, R * k:R * k + R], a_rows[t % 4][:, R * k:R * k + R], ident[:])
                last.then_inc(at_ps, 1)

            def embed(b, t):
                u = t % 2
                n = b * T + t
                pe.wait_ge(at_lo, n + 1)
                pe.wait_ge(h_set, n + 1)
                for c in range(4):
                    dst = ps[:, 2 + 2 * u + c // 2, 256 * (c % 2):256 * (c % 2) + 256]
                    terms = [(l, r) for k in range(3) for l, r in halves(
                        a_t[u][:, 0, R * k:R * k + R], a_t[u][:, 1, R * k:R * k + R],
                        b_w[:, c, 0, 256 * k:256 * k + 256], b_w[:, c, 1, 256 * k:256 * k + 256])]
                    for k, (l, r) in enumerate(terms):
                        last = mm_(dst, l, r, start=k == 0, stop=k == len(terms) - 1)
                last.then_inc(emb_ps, 1)

            turn_rows(0, 0)
            turn_rows(0, 1)
            pe.wait_ge(w_lo, C_V + 2)
            embed(0, 0)
            embed(0, 1)
            with pe.Fori(0, B) as b:
                pe.wait_ge(f_set, b * T + 1)
                turn_rows(b, 2)
                for t in range(2, T):
                    if t < T - 1:
                        turn_rows(b, t + 1)
                    embed(b, t)
                    if t == 2:
                        pe.wait_ge(f_set, b * T + 2)
                    turn_stream(b * 2, t - 2, 6, 1)
                pe.wait_ge(w_lo, b * NCHUNK + C_M + 2)
                for t in range(T):
                    if t == 2:
                        pe.wait_ge(h_set, (b + 1) * T + 2)
                    pe.wait_ge(y_lo, b * 2 * T + t + 3)
                    pe.wait_ge(v_set, b * T + t + 1)
                    wv = ((hi(3), lo(3)), (kst[:, 0, :], kst[:, 1, :]))
                    terms = [(l, r) for k in range(KT) for l, r in halves(
                        x_hi[:, k, P * t:P * t + P], x_lo[:, k, P * t:P * t + P],
                        *(w[:, 256 * (k % 4):256 * (k % 4) + 256] for w in wv[k // 4]))]
                    for k, (l, r) in enumerate(terms):
                        last = mm_(ps[:, V_BANKS[t % 4], 0:256], l, r, start=k == 0, stop=k == len(terms) - 1)
                    last.then_inc(v_ps, 1)
                    if t in V_TURNS:
                        turn_stream(b * 2, V_TURNS[t], 6, 1)
                gate(v_set, b * T + 6 + 4)
                def projection(m, u, hf, uses=()):
                    r = (b * MT + m) * 2 + hf
                    pe.wait_ge(p_lo, r + 1)
                    terms = [(l, rr) for k in range(KT) for l, rr in halves(
                        hi(2 + u)[:, P * k:P * k + P], lo(2 + u)[:, P * k:P * k + P],
                        x_hi[:, k, H * hf:H * hf + H], x_lo[:, k, H * hf:H * hf + H])]
                    for k, (l, rr) in enumerate(terms):
                        last = mm_(ps[:, 2 * u + hf, :], l, rr, start=k == 0, stop=k == len(terms) - 1)
                        if k % 6 == 2 and k // 6 < len(uses):
                            maximum(0, 0, uses[k // 6], 0)
                    last.then_inc(p_ps, 1)

                def maximum(g, u, k, half):
                    gi = b * NKV + g
                    bank = ps[:, 6 + k % 2, :]
                    if USES[k][0] == "P":
                        _, qt, kh, w, j0, heads = USES[k]
                        n = before(k)
                        if n == 0:
                            pe.wait_ge(qk_in[u][0], (b * (NKV // 2) + half + 1) * 96)
                        if n == FIRST:
                            pe.wait_ge(qk_in[u][1], (b * (NKV // 2) + half + 1) * 96)
                        pe.wait_ge(mx_rd, gi * NUSE + k + 1)
                        for j in range(heads):
                            last = mm_(bank[:, w * j:w * j + w], ring[0:96, 4 * u + j0 + j, P * qt:P * qt + P], kst[0:96, u, H * kh:H * kh + w],
                                       start=True, stop=True)
                        if kh == qt // 4:
                            for j in range(heads):
                                last = mm_(bank[:, w * j + w - P:w * j + w], ident_r[:], causal[:], start=False, stop=True, skip_group_check=True)
                        last.then_inc(mx_ps, 1)
                    else:
                        x = USES[k][1]
                        pe.wait_ge(m_neg, gi * 2 + x + 1)
                        pe.wait_ge(mx_rd, gi * NUSE + k + 1)
                        nc.tensor.transpose(bank[0:MROWS, 0:P], negm[:, u, x, :], ident[:]).then_inc(m_ps, 1)

                with pe.Fori(0, 2) as mm:
                    for u in range(2):
                        pe.wait_ge(w_lo, b * NCHUNK + C_M + mm * 2 + u + 1 + 2)
                        for hf in range(2):
                            projection(mm * 2 + u, u, hf)
                pe.wait_ge(y_lo, (b * 2 + 1) * T + 2)
                pe.wait_ge(v_set, (b + 1) * T + 4)
                for n in range(12):
                    m, u, hf = 4 + n // 2, n // 2 % 2, n % 2
                    if hf == 0:
                        pe.wait_ge(w_lo, b * NCHUNK + C_M + m + 1 + 2)
                    projection(m, u, hf, START[n])
                pe.wait_ge(p_cos, (b + 1) * (2 * MT))
                gate(k_ones, b + 1)

                def scores(g, u, n, own, half):
                    gi = b * NKV + g
                    kt = STEPS[n][1]
                    q0, w = step_range(n)
                    if half == 0 and n in (0, 4):
                        pe.wait_ge(m_in[n // 4], (gi + 1) * 32)
                    if half == 0 and n == 4:
                        pe.wait_ge(qk_in[u][1], (b * (NKV // 2) + own + 1) * 96)
                    if half == 0:
                        pe.wait_ge(e_set, gi * NSTEP + n + 1)
                    for j in (2 * half, 2 * half + 1):
                        last = mm_(ps[:, j, 0:w], kst[0:98, u, P * kt:P * kt + P], ring[0:98, 4 * u + j, q0:q0 + w], start=True, stop=True)
                    if half == 1:
                        last.then_inc(st_ps, 1)

                def weighted(g, u, n, sums):
                    gi = b * NKV + g
                    qh, kt = STEPS[n]
                    q0, w = step_range(n)
                    c0 = q0 - H * qh
                    if not sums:
                        if n == 0:
                            pe.wait_ge(vg_set, gi + 1)
                        if kt == 0:
                            pe.wait_ge(o_nm, gi * 2 + qh + 1)
                        pe.wait_ge(e_set, gi * NSTEP + n + 2)
                        if n in DIAG:
                            pe.wait_ge(e_mask, gi * len(DIAG) + DIAG.index(n) + 1)
                    bank, lhs = (5, ones[:]) if sums else (4, vg[:, u, kt, :])
                    for j in range(GQ):
                        last = mm_(ps[HD * j:HD * j + HD, bank, c0:c0 + w], lhs, work[:, n % 3, j, 0:w],
                                   start=kt == 0, stop=kt == 4 * qh + 3, skip_group_check=True)
                    if sums and kt == 4 * qh + 3:
                        last.then_inc(o_ps, 1)

                def group(g, u, own, half, first=False, last=False):
                    for n in range(NSTEP):
                        todo = list(PLAN[first][n])

                        def maxima():
                            for k in todo.pop(0):
                                if not last:
                                    maximum(g + 1, 1 - u, k, half)

                        for pair in range(2):
                            maxima()
                            scores(g, u, n, own, pair)
                        for m in WEIGHTED[n]:
                            for sums in (False, True):
                                maxima()
                                if m >= 0:
                                    weighted(g, u, m, sums)
                                elif not first:
                                    weighted(g - 1, 1 - u, NSTEP + m, sums)
                        maxima()

                group(0, 0, 0, 0, first=True)
                with pe.Fori(0, 3) as gg:
                    group(gg * 2 + 1, 1, gg, gg + 1)
                    group(gg * 2 + 2, 0, gg + 1, gg + 1)
                group(7, 1, 3, 4, last=True)
                for n in (NSTEP - 2, NSTEP - 1):
                    weighted(7, 1, n, False)
                    weighted(7, 1, n, True)

                gate(o_lo, (b + 1) * (2 * NKV) + 1)
                def output(n, nu, t, bank, read):
                    pe.wait_ge(op_set, b * 4 * T + read + 8)
                    terms = [(l, r) for k in range(KT) for l, r in halves(
                        x_hi[:, k, P * t:P * t + P], x_lo[:, k, P * t:P * t + P],
                        hi(2 * nu + k // 4)[:, 256 * (k % 4):256 * (k % 4) + 256],
                        lo(2 * nu + k // 4)[:, 256 * (k % 4):256 * (k % 4) + 256])]
                    for k, (l, r) in enumerate(terms):
                        last = mm_(ps[:, bank, 0:256], l, r, start=k == 0, stop=k == len(terms) - 1)
                    last.then_inc(op_ps, 1)

                for n in range(2):
                    pe.wait_ge(w_lo, b * NCHUNK + C_O + n * 2 + 2 + 2)
                    for t in range(T):
                        if n == 0 and t == 4:
                            pe.wait_ge(o_lo, (b + 1) * (2 * NKV) + 2)
                        output(n, n, t, t, n * T + t - 7)
                pe.wait_ge(w_lo, b * NCHUNK + C_O + 6 + 2)
                for i, (n, t) in enumerate(LAST):
                    if i == 3:
                        pe.wait_ge(w_lo, b * NCHUNK + C_O + 8 + 2)
                    output(n, n % 2, t, i % 4, T + i + 1 if i < 4 else 2 * T + i - 3)
                    if n == 3 and t >= 2:
                        if t == 2:
                            pe.wait_ge(op_set, (b * 4 + 2) * T + 8)
                        turn_stream(b * 2 + 1, t - 2, 4 + 2 * (t % 2), 2)
                for t in (T - 2, T - 1):
                    turn_stream(b * 2 + 1, t, 4 + 2 * (t % 2), 2)
                pe.wait_ge(y_lo, (b * 2 + 2) * T + 2)
                pe.wait_ge(down_in, (b + 1) * 16)
                def up(pp, hf):
                    for e in range(2):
                        hh = 2 * pp + e
                        if hf == 0 and hh % 4 == 0:
                            pe.wait_ge(w_lo, b * NCHUNK + C_U + hh // 4 + 1 + 2)
                        if hf == 0:
                            pe.wait_ge(t_in[hh % 4], (b * (FH // 4) + hh // 4 + 1) * 16)
                        pe.wait_ge(gel_set, (b * (FH // 2) + pp) * 4 + 2 * hf + e + 1)
                        for m in range(2):
                            w0 = FM * (hh % 4) + P * m
                            for k, w in enumerate((hi(hh // 4), lo(hh // 4))):
                                last = mm_(ps[:, 2 * e + m, :], w[:, w0:w0 + P], x_lo[:, hh % 4, H * hf:H * hf + H], start=k == 0, stop=k == 1)
                        last.then_inc(up_ps, 1)

                def downward(pp, hf):
                    n = (b * (FH // 2) + pp) * 2 + hf
                    pe.wait_ge(dn_set, n + 1)
                    pe.wait_ge(gel_set, (b * (FH // 2) + pp) * 4 + 2 * hf + 4)
                    for m in range(2):
                        for e in range(2):
                            w0 = ((2 * pp + e) * 2 + m) * FD
                            last = mm_(ps[FD * e:FD * e + FD, 4 + 2 * (pp % 2) + hf, :], down_sb[:, w0:w0 + FD],
                                       gel[:, 2 * hf + e, m, :], start=m == 0, stop=m == 1, skip_group_check=True)
                    last.then_inc(dn_ps, 1)

                for pp in range(FH // 2):
                    up(pp, 0)
                    if pp:
                        downward(pp - 1, 1)
                    up(pp, 1)
                    downward(pp, 0)
                pe.wait_ge(gel_set, (b + 1) * (2 * FH) + 1)
                turn_rows(b + 1, 0)
                turn_rows(b + 1, 1)
                downward(FH // 2 - 1, 1)
                pe.wait_ge(w_lo, (b + 1) * NCHUNK + C_V + 2)
                pe.wait_ge(dn_set, (b + 1) * FH + 2)
                embed(b + 1, 0)
                embed(b + 1, 1)
                pe.wait_ge(at_lo, (b + 1) * T + 2)
                pe.wait_ge(dn_set, (b + 1) * FH + 4)
                for t in range(T):
                    if t % 2 == 0:
                        pe.wait_ge(z_in[t // 2], (b + 1) * 16)
                    pe.wait_ge(f_set, b * T + t + 1)
                    for k in range(KT):
                        last = nc.tensor.transpose(ps[:, F_PAIRS[t % 2] + k // 4, P * (k % 4):P * (k % 4) + P], z_sb[:, k, P * t:P * t + P], ident[:])
                    last.then_inc(f_ps, 1)


def _tiles(w, rows):
    k, n = w.shape[0] // P, w.shape[1] // rows
    return w.reshape(k, P, n, rows).transpose(2, 1, 0, 3).reshape(n, P, k * rows)


def kernel(**inputs):
    import numpy as np
    import concourse.bacc as bacc
    from concourse.bass_utils import run_bass_kernel_spmd as run

    a = {k: np.asarray(v) for k, v in inputs.items()}

    def columns(x):
        return np.ascontiguousarray(x.reshape(B * T, P).T)

    pairs = np.arange(HD).reshape(2, HD // 2).T.reshape(-1)

    def paired(w):
        return w.reshape(-1, HD, D)[:, pairs, :].reshape(-1, D)

    lora_b = np.stack([a["L0_tok_lora_B_cl"], a["L0_tok_lora_B_lm"], a["L0_tok_lora_B_cl_prime"]], 1)
    b_chunks = np.zeros((4, P, 1024), np.float32)
    b_chunks[:, :, 0:768] = lora_b.reshape(R, 3, 4, 256).transpose(2, 0, 1, 3).reshape(4, R, 768)
    wv = a["L0_attn_Wv"].T.reshape(2, 4, P, 256).transpose(0, 2, 1, 3).reshape(2, P, 1024)
    wk = _tiles(paired(a["L0_attn_Wk"]).T, P)
    wq = _tiles(paired(a["L0_attn_Wq"]).T, P)
    wo = a["L0_attn_Wo"].T.reshape(2, 4, P, 4, 256).transpose(3, 0, 2, 1, 4).reshape(8, P, 1024)
    up = a["L0_ffn_up"].reshape(4, 4, FD, FM).transpose(0, 2, 1, 3).reshape(4, FD, 4 * FM)
    up = np.concatenate([up, up], 1)
    chunks = np.concatenate([b_chunks, wv, wk, wq, wo, up], 0)
    down = a["L0_ffn_down"].reshape(FH, 2, P, FD).transpose(2, 0, 1, 3).reshape(P, FH * 2 * FD)

    inv = (np.float32(1.0) / np.float32(10000.0) ** (np.arange(0, HD, 2, dtype=np.float32) / np.float32(HD))).astype(np.float32)
    ang = np.outer(np.arange(S, dtype=np.float32), inv).astype(np.float32)
    cos = np.tile(np.repeat(np.cos(ang).T, 2, 0), (4, 1)).astype(np.float32)
    sin = (np.tile(np.repeat(np.sin(ang).T, 2, 0), (4, 1)) * np.tile(np.array([[1.0], [-1.0]]), (64, 1))).astype(np.float32)

    perm = a["L0_ffn_perm"]
    perm_up = np.tile(perm.reshape(FH, FD), (1, 2)).T
    perm_down = perm.reshape(FH // 2, P).T
    arrays = {
        "ids": columns(a["x"]), "mask1": columns(a["mask_BS_i1_0"]), "mask0": columns(a["mask_BS_i0_1"]),
        "table_w": a["L0_tok_weight"], "table_a1": a["L0_tok_lora_A_cl"],
        "table_a23": np.concatenate([a["L0_tok_lora_A_lm"], a["L0_tok_lora_A_cl_prime"]], 1),
        "chunks": chunks, "down": down, "cos": cos, "sin": sin, "perm_up": perm_up, "perm_down": perm_down,
    }
    nc = bacc.Bacc("TRN2", target_bir_lowering=False, num_devices=1)
    feeds, aps = {}, []
    for name, arr in arrays.items():
        arr = np.ascontiguousarray(arr)
        feeds[f"{name}_dram"] = arr
        aps.append(nc.dram_tensor(f"{name}_dram", arr.shape, mybir.dt.from_np(arr.dtype), kind="ExternalInput").ap())
    out = nc.dram_tensor("out_dram", (B * S, D), F32, kind="ExternalOutput").ap()
    program(nc, *aps, out)
    r = run(nc, [feeds], core_ids=[0])
    return r.results[0]["out_dram"].reshape(B, S, D)
```
